# Optimizing a Trainium2 kernel written in Bass

```python
import numpy as np
import jax
import jax.numpy as jnp

def _softmax(x, axis=-1):
    return jax.nn.softmax(x, axis=axis)

def _gelu(x):
    return jax.nn.gelu(x, approximate=True)

def _silu(x):
    return jax.nn.silu(x)

def _sigmoid(x):
    return jax.nn.sigmoid(x)

def _layernorm(x, axis=-1, eps=1e-05):
    m = jnp.mean(x, axis=axis, keepdims=True)
    v = jnp.var(x, axis=axis, keepdims=True)
    return (x - m) / jnp.sqrt(v + eps)

def _scatter_add(tgt, idx, src, axis=0):
    return tgt.at[idx].add(src)

def _segment_sum(src, seg, n):
    return jax.ops.segment_sum(src, seg, n)
kernel_name = 'mk_seq_postln_d1_jaxref_r8_3904c6'

def setup_inputs(seed: int=0):
    np.random.seed(seed)
    _w = jnp.asarray

    def _L0_attn_setup():
        import jax, jax.numpy as jnp
        import numpy as np
        D_MODEL, N_HEADS, BATCH, SEQ = (128, 16, 2, 256)

        def get_freqs(seq, n_dim):
            inv_freq = 1.0 / 10000.0 ** (jnp.arange(0, n_dim, 2, dtype=jnp.float32) / n_dim)
            pos = jnp.arange(seq, dtype=jnp.float32)
            return pos[:, None] * inv_freq[None, :]

        def rope(x, freq):
            cos = jnp.cos(freq)[None, :, None, :]
            sin = jnp.sin(freq)[None, :, None, :]
            x1, x2 = (x[..., ::2], x[..., 1::2])
            r1 = x1 * cos - x2 * sin
            r2 = x1 * sin + x2 * cos
            return jnp.stack([r1, r2], axis=-1).reshape(x.shape)
        key = jax.random.key(seed)
        ks = jax.random.split(key, 5)
        w_scale = 0.01
        return {'x': jax.random.normal(ks[0], (BATCH, SEQ, D_MODEL), dtype=jnp.float32), 'qw': jax.random.normal(ks[1], (D_MODEL, D_MODEL), dtype=jnp.float32) * w_scale, 'kw': jax.random.normal(ks[2], (D_MODEL, D_MODEL), dtype=jnp.float32) * w_scale, 'vw': jax.random.normal(ks[3], (D_MODEL, D_MODEL), dtype=jnp.float32) * w_scale, 'ow': jax.random.normal(ks[4], (D_MODEL, D_MODEL), dtype=jnp.float32) * w_scale}
    _L0_attn_in = _L0_attn_setup()

    def _L0_ffn_setup():
        import jax, jax.numpy as jnp
        import numpy as np
        B, S, D, F, E, K = (4, 256, 128, 512, 4, 2)
        key = jax.random.key(seed)
        k = jax.random.split(key, 6)
        x = jax.random.normal(k[0], (B, S, D), jnp.float32)
        router_w = jax.random.normal(k[1], (D, E), jnp.float32) * D ** (-0.5)
        router_b = jnp.zeros((E,), jnp.float32)
        w1 = jax.random.normal(k[2], (E, D, F), jnp.float32) * 0.02
        w3 = jax.random.normal(k[3], (E, D, F), jnp.float32) * 0.02
        w2 = jax.random.normal(k[4], (E, F, D), jnp.float32) * 0.02
        return {'x': x, 'router_w': router_w, 'router_b': router_b, 'w1': w1, 'w3': w3, 'w2': w2}
    _L0_ffn_in = _L0_ffn_setup()
    _d = {'L0_attn_x': _L0_attn_in['x'], 'L0_attn_qw': _L0_attn_in['qw'], 'L0_attn_kw': _L0_attn_in['kw'], 'L0_attn_vw': _L0_attn_in['vw'], 'L0_attn_ow': _L0_attn_in['ow'], 'L0_ffn_router_w': _L0_ffn_in['router_w'], 'L0_ffn_router_b': _L0_ffn_in['router_b'], 'L0_ffn_w1': _L0_ffn_in['w1'], 'L0_ffn_w3': _L0_ffn_in['w3'], 'L0_ffn_w2': _L0_ffn_in['w2']}
    _x0 = _d['L0_attn_x']
    _d['L0_attn_x'] = jax.random.normal(jax.random.fold_in(jax.random.key(seed), 1), (2, 1024, 128), dtype=_x0.dtype)
    del _x0
    return _d

def reference(L0_attn_x, L0_attn_qw, L0_attn_kw, L0_attn_vw, L0_attn_ow, L0_ffn_router_w, L0_ffn_router_b, L0_ffn_w1, L0_ffn_w3, L0_ffn_w2):

    def _L0_attn_ref(x, qw, kw, vw, ow):
        import jax, jax.numpy as jnp
        import numpy as np
        D_MODEL, N_HEADS, BATCH, SEQ = (128, 16, 2, 256)

        def get_freqs(seq, n_dim):
            inv_freq = 1.0 / 10000.0 ** (jnp.arange(0, n_dim, 2, dtype=jnp.float32) / n_dim)
            pos = jnp.arange(seq, dtype=jnp.float32)
            return pos[:, None] * inv_freq[None, :]

        def rope(x, freq):
            cos = jnp.cos(freq)[None, :, None, :]
            sin = jnp.sin(freq)[None, :, None, :]
            x1, x2 = (x[..., ::2], x[..., 1::2])
            r1 = x1 * cos - x2 * sin
            r2 = x1 * sin + x2 * cos
            return jnp.stack([r1, r2], axis=-1).reshape(x.shape)
        batch, seq, dim = x.shape
        n_heads = N_HEADS
        n_dim = dim // n_heads
        Q = (x @ qw).astype(jnp.float32).reshape(batch, seq, n_heads, n_dim)
        K = (x @ kw).astype(jnp.float32).reshape(batch, seq, n_heads, n_dim)
        V = (x @ vw).astype(jnp.float32).reshape(batch, seq, n_heads, n_dim)
        freq = get_freqs(seq, n_dim)
        Q = rope(Q, freq)
        K = rope(K, freq)
        Q = jnp.transpose(Q, (0, 2, 1, 3))
        K = jnp.transpose(K, (0, 2, 1, 3))
        V = jnp.transpose(V, (0, 2, 1, 3))
        scale = jnp.sqrt(jnp.float32(n_dim))
        score = jnp.einsum('bhqd,bhkd->bhqk', Q, K) / scale
        causal = jnp.tril(jnp.ones((1, 1, seq, seq), dtype=jnp.float32))
        score = score - 10000000000.0 * (1.0 - causal)
        score = score - jnp.max(score, axis=-1, keepdims=True)
        weights = jax.nn.softmax(score, axis=-1)
        attn = jnp.einsum('bhqk,bhkd->bhqd', weights, V)
        merged = jnp.transpose(attn, (0, 2, 1, 3)).reshape(batch, seq, dim)
        return (merged @ ow).astype(x.dtype)

    def _L0_ffn_ref(x, router_w, router_b, w1, w3, w2):
        import jax, jax.numpy as jnp
        import numpy as np
        B, S, D, F, E, K = (4, 256, 128, 512, 4, 2)
        b, s, d = x.shape
        T = b * s
        e = router_w.shape[1]
        xf = x.reshape(T, d)
        logits = xf @ router_w + router_b
        probs = jax.nn.softmax(logits, axis=-1)
        top_p, top_i = jax.lax.top_k(probs, K)
        top_p = top_p / jnp.sum(top_p, axis=-1, keepdims=True)
        gates = jnp.zeros((T, e), xf.dtype).at[jnp.arange(T)[:, None], top_i].add(top_p)
        h = jax.nn.silu(jnp.einsum('td,edf->etf', xf, w1)) * jnp.einsum('td,edf->etf', xf, w3)
        expert_out = jnp.einsum('etf,efd->etd', h, w2)
        out = jnp.einsum('te,etd->td', gates, expert_out)
        return out.reshape(b, s, d)
    x = L0_attn_x
    x = _layernorm(x + _L0_attn_ref(x, L0_attn_qw, L0_attn_kw, L0_attn_vw, L0_attn_ow), axis=-1)
    x = _layernorm(x + _L0_ffn_ref(x, L0_ffn_router_w, L0_ffn_router_b, L0_ffn_w1, L0_ffn_w3, L0_ffn_w2), axis=-1)
    return x

_drawn_inputs = setup_inputs


def setup_inputs(seed=0):
    import zlib

    import numpy as np

    out = dict(_drawn_inputs(seed))
    spreads = {'L0_ffn_router_b': (0.0, 0.8)}
    factors = {'L0_attn_qw': 8.0,
     'L0_attn_kw': 8.0,
     'L0_attn_vw': 8.0,
     'L0_attn_ow': 8.0,
     'L0_ffn_router_w': 8.0,
     'L0_ffn_w1': 6.408,
     'L0_ffn_w3': 6.392,
     'L0_ffn_w2': 6.372}
    for name, (base, spread) in spreads.items():
        noise = np.random.default_rng([zlib.crc32(name.encode()), seed]).standard_normal(out[name].shape)
        drawn = base * np.exp(spread * noise) if base else spread * noise
        out[name] = jnp.asarray(drawn.astype(out[name].dtype))
    for name, factor in factors.items():
        out[name] = (out[name] * factor).astype(out[name].dtype)
    return out
```

```python
from contextlib import ExitStack

import numpy as np

import concourse.bass as bass
from concourse import mybir

F32 = mybir.dt.float32
F32R = mybir.dt.float32r
BF16 = mybir.dt.bfloat16
ALU = mybir.AluOpType
ACT = mybir.ActivationFunctionType
AX = mybir.AxisListType

P = 128
B, S, D = 2, 1024, 128
H = 16
DH = D // H
E, F = 4, 512
T = B * S
EPS = 1e-5

GH = 4
QD = P // GH
NG = H // GH
GROUPS = B * NG
CH = 512
NC = S // CH
CHUNKS = T // CH
TI = CH // P
NB = CH // QD
KT = S // P
QROWS = 3 * DH + 2
KROWS = 3 * DH
MASKED = -1e30
FT = F // P
UNITS = E * FT

S_UNITS = [(0, j, 0) for j in range(CH // QD)]
S_UNITS += [(1, j, half) for j in range(CH // QD, S // QD) for half in range(2)]
T_UNITS = [(c, kt, h) for c in range(NC) for kt in range(TI * (c + 1)) for h in range(GH)]
NS = len(S_UNITS)
NT = len(T_UNITS)
SEG_S = [sum(u[0] == c for u in S_UNITS) for c in range(NC)]
SEG_T = [sum(u[0] == c for u in T_UNITS) for c in range(NC)]
NPV = NT // GH
SB = 3
TB = 3
HB = 4
PB = 3


def stage_plan(with_s, with_t):
    plan = []
    for c in range(NC):
        s_units = [u for u in S_UNITS if u[0] == c] if with_s else []
        t_units = [u for u in T_UNITS if u[0] == c] if with_t else []
        kept = 6 if c == NC - 1 and with_t else 0
        steps = max(SEG_S[c], SEG_T[c])
        done_s = 0
        for x in range(steps):
            if x < len(t_units):
                plan.append(("T", *t_units[x]))
            want = (x + 1) * (len(s_units) - kept) // steps
            while s_units and done_s < want:
                plan.append(("S", *s_units[done_s]))
                done_s += 1
            if with_t and x % GH == GH - 1:
                kt = x // GH
                if kt >= 1:
                    plan.append(("PV", c, kt - 1))
                elif c > 0:
                    plan.append(("PV", c - 1, TI * c - 1))
                    plan.append(("OCOPY", c - 1))
            if x == 5:
                if c > 0 and with_s:
                    plan.append(("MROWS", c - 1))
                if c == 0 and with_t:
                    plan.append(("MROWS", NC - 1))
            if x == 11 and with_t:
                plan.append(("NORM", (c - 1) % NC))
        if c == NC - 1 and with_t:
            while s_units and done_s < len(s_units):
                plan.append(("S", *s_units[done_s]))
                done_s += 1
            plan.append(("PV", c, TI * (c + 1) - 1))
            plan.append(("OCOPY", c))
        plan.append(("END", c))
    if with_t and not with_s:
        plan.append(("NORM", NC - 1))
    uses = iter(range(len(plan)))
    return [(*step, next(uses)) if step[0] in ("MROWS", "NORM") else step for step in plan]


PROLOGUE = stage_plan(True, False)
STEADY = stage_plan(True, True)
LAST = stage_plan(False, True)
SMALL_0 = sum(x[0] in ("MROWS", "NORM") for x in PROLOGUE)
SMALL = sum(x[0] in ("MROWS", "NORM") for x in STEADY)
PIECE = 3 * E * F // (GROUPS - 2)
assert NS % SB == 0 and NT % TB == 0 and NPV % PB == 0


EO_STEP, TR_STEP, Y_STEP = FT + 2, FT + 3, FT + 4
FFN_STEPS = Y_STEP + UNITS


def transformer_block(nc, x_tok, x_feat, qw, kw, vw, ow, router_w, router_b, w_all,
                      cos_t, sin_t, ident_d, mask_d, tri_d, out):
    nc.disable_value_cache = True
    ctx = ExitStack()
    with ctx:
        def sb(name, shape, dt=F32):
            return ctx.enter_context(nc.sbuf_tensor(name, shape, dt))

        def sem(name):
            return ctx.enter_context(nc.semaphore(name))

        bank = [ctx.enter_context(nc.psum_tensor(f"bank{i}", [P, CH], F32)) for i in range(8)]
        s_bank, t_bank, o_bank, small_bank = bank[0:3], bank[3:6], bank[6], bank[7]

        q_dram = nc.dram_tensor("q_scratch", (B * H, QROWS, S), F32).ap()
        k_dram = nc.dram_tensor("k_scratch", (B * H, KROWS, S), F32).ap()
        v_dram = nc.dram_tensor("v_scratch", (GROUPS, P, KT, GH * QD), F32).ap()

        cos_sb, sin_sb = sb("cos_sb", [P, S]), sb("sin_sb", [P, S])
        ident = sb("ident", [P, P])
        mask_f = sb("mask_f", [P, QD])
        ident_b, mask_b = sb("ident_b", [P, P], BF16), sb("mask_b", [P, QD], BF16)
        tri = sb("tri", [P, 2, E * E])
        wqk = sb("wqk", [P, 4, D])
        wv, wo = sb("wv", [P, D]), sb("wo", [P, D])
        rw, rb = sb("rw", [P, E]), sb("rb", [P, E])
        xT = sb("xT", [P, T])
        x_res = sb("x_res", [P, T // P, D])
        w_raw = sb("w_raw", [P, PIECE])
        w_hi, w_lo = sb("w_hi", [P, 3 * E * F], F32R), sb("w_lo", [P, 3 * E * F], F32R)

        by_cos, by_sin = sb("by_cos", [P, 2, CH]), sb("by_sin", [P, 2, CH])
        roped = sb("roped", [P, 2, CH])
        rope_hi, rope_lo = sb("rope_hi", [P, 2, CH]), sb("rope_lo", [P, 2, CH])

        q_op = [sb(f"q_op{u}", [P, S // QD, GH, QD], F32R) for u in range(2)]
        k_op = [sb(f"k_op{u}", [P, S], F32R) for u in range(2)]
        v_op = [sb(f"v_op{u}", [P, KT, GH, QD]) for u in range(2)]
        num = sb("num", [P, PB, GH, CH])
        maxima = sb("maxima", [P, 2, S // QD])
        neg_max = [sb(f"neg_max{c}", [P, 2 * CH // QD]) for c in range(NC)]
        max_rows = [sb(f"max_rows{c}", [2 * CH // QD, P]) for c in range(NC)]
        o_sb = [sb(f"o_sb{c}", [P, CH]) for c in range(NC)]
        rden = sb("rden", [P, TI, GH])
        merged = sb("merged", [P, GROUPS + 1, S // P, QD])
        v_stage = num[:, :, :, :].rearrange("p a b c -> p (a b c)")[:, 0:KT * H * QD]\
            .rearrange("p (k h r) -> p k h r", k=KT, h=H)

        mg_w, mg_t, x1_w, x1_tw = (sb(n, [P, CH]) for n in ("mg_w", "mg_t", "x1_w", "x1_tw"))
        resid = sb("resid", [P, CH])
        x1 = sb("x1", [P, T // P, D])
        flat = [q_op[u][:, :, :, :].rearrange("p j h q -> p (j h q)") for u in range(2)]
        x1_hi, x1_lo = flat[0][:, 0:T], flat[0][:, T:2 * T]
        stats, mv = sb("stats", [P, TI, 6]), sb("mv", [P, TI, 2])
        veps, rstd, minus_half = sb("veps", [P, TI]), sb("rstd", [P, TI]), sb("minus_half", [P, TI])
        logits = sb("logits", [P, TI, E])
        gt, ge = sb("gt", [P, TI, E, E]), sb("ge", [P, TI, E, E])
        rank, chosen = sb("rank", [P, TI, E]), sb("chosen", [P, TI, E])
        top, expd, gsum = sb("top", [P, TI]), sb("expd", [P, TI, E]), sb("gsum", [P, TI])
        gates = sb("gates", [P, T // P, E])
        hid_hi, hid_lo = (flat[1][:, i * HB * CH:(i + 1) * HB * CH].rearrange("p (n t) -> p n t", n=HB)
                          for i in range(2))
        hid, silu_sb, eo_sb = num[:, 0, :, :], num[:, 1, 0:2, :], num[:, 1, 2:4, :]
        y_sb, z_sb = (num[:, 2, i, :].rearrange("p (i d) -> p i d", i=TI) for i in range(2))

        ld_proj, ld_tab, ld_x, ld_res, ld_small = (sem(n) for n in (
            "ld_proj", "ld_tab", "ld_x", "ld_res", "ld_small"))
        ld_w = sem("ld_w")
        zeros_stored = sem("zeros_stored")
        ops_filled = sem("ops_filled")
        q_loaded = [[sem(f"q_loaded{u}{c}") for c in range(NC)] for u in range(2)]
        k_loaded = [[sem(f"k_loaded{u}{c}") for c in range(NC)] for u in range(2)]
        v_loaded = [sem(f"v_loaded{u}") for u in range(2)]
        rot_ready, proj_ready, turned, roped_ready, hi_ready, lo_ready = (sem(n) for n in (
            "rot_ready", "proj_ready", "turned", "roped_ready", "hi_ready", "lo_ready"))
        hilo_stored = [sem(f"hilo_stored{i}") for i in range(2)]
        v_proj, v_cleared, v_copied, v_stored = (sem(n) for n in ("v_proj", "v_cleared", "v_copied", "v_stored"))
        s_ready, s_reduced = sem("s_ready"), sem("s_reduced")
        t_ready, t_exped = sem("t_ready"), sem("t_exped")
        masked, pv_done, o_copied = sem("masked"), sem("pv_done"), sem("o_copied")
        max_split, small_ready, small_read = sem("max_split"), sem("small_ready"), sem("small_read")
        rows_loaded = [sem(f"rows_loaded{c}") for c in range(NC)]
        dve_step, dve_turn, pool_turn = sem("dve_step"), sem("dve_turn"), sem("pool_turn")
        w_split, w_hi_done, small_cast = sem("w_split"), sem("w_hi_done"), sem("small_cast")
        c_mg, c_mgt, c_mgs, c_y, c_var, c_rstd, c_x1, c_x1t, c_x1s, c_hi, c_log, c_lo, c_exp, c_store, c_top = (
            sem(n) for n in ("c_mg", "c_mgt", "c_mgs", "c_y", "c_var", "c_rstd", "c_x1", "c_x1t", "c_x1s",
                             "c_hi", "c_log", "c_lo", "c_exp", "c_store", "c_top"))
        c_done = sem("c_done")
        f_ab, f_silu, f_hid, f_hi, f_lo, f_eo, f_tr, f_y = (sem(n) for n in (
            "f_ab", "f_silu", "f_hid", "f_hi", "f_lo", "f_eo", "f_tr", "f_y"))
        f_w2 = sem("f_w2")
        f_var, f_rstd, f_z = sem("f_var"), sem("f_rstd"), sem("f_z")
        out_stored = sem("out_stored")

        block = ctx.enter_context(nc.Block())

        @block.sync
        def _(sp):
            sp.sem_inc(out_stored, 16)
            for w, i in ((qw, 0), (kw, 2)):
                sp.dma_start(wqk[:, i, :], w).then_inc(ld_proj, 16)
            sp.dma_start(wv[:, :], vw).then_inc(ld_proj, 16)
            for ch in range(CHUNKS):
                sp.dma_start(xT[:, ch * CH:(ch + 1) * CH], x_feat[:, ch * CH:(ch + 1) * CH]).then_inc(ld_x, 16)
                if ch == 0:
                    sp.dma_start(cos_sb[:, :], cos_t).then_inc(ld_tab, 16)
                    sp.dma_start(sin_sb[:, :], sin_t).then_inc(ld_tab, 16)
                sp.wait_ge(ld_x, 16 * (ch + 1))
            for dst, src in ((ident[:, :], ident_d), (mask_f[:, :], mask_d), (wo[:, :], ow), (rw[:, :], router_w),
                             (tri[:, :, :], tri_d), (rb[:, :], router_b.partition_broadcast(P))):
                sp.dma_start(dst, src).then_inc(ld_small, 16)
            sp.wait_ge(ops_filled, 1)
            sp.dma_start(q_dram[:, KROWS:QROWS, :],
                         flat[0][0:B * H * 2, 0:S].bitcast(F32))\
                .then_inc(zeros_stored, 16)
            for n in range(2 * CHUNKS):
                ch, is_k = divmod(n, 2)
                b, c = divmod(ch, NC)
                cols = slice(c * CH, (c + 1) * CH)
                heads = slice(b * H, (b + 1) * H)
                dram = k_dram if is_k else q_dram
                hi_at, lo_at = ((0, 2), 1) if is_k else ((0, 1), 2)
                sp.wait_ge(hi_ready, n + 1)
                for r in hi_at:
                    sp.dma_start(dram[heads, r * DH:(r + 1) * DH, cols],
                                 rope_hi[:, n % 2, :])\
                        .then_inc(hilo_stored[n % 2], 16)
                sp.wait_ge(lo_ready, n + 1)
                sp.dma_start(dram[heads, lo_at * DH:(lo_at + 1) * DH, cols],
                             rope_lo[:, n % 2, :])\
                    .then_inc(hilo_stored[n % 2], 16)
                if is_k and c == NC - 1:
                    sp.wait_ge(v_copied, NC * (b + 1))
                    for g in range(NG):
                        sp.dma_start(v_dram[b * NG + g],
                                     v_stage[:, :, g * GH:(g + 1) * GH, :].rearrange("p k h r -> p k (h r)"))\
                            .then_inc(v_stored, 16)

            def load_q(n, u, c):
                for h in range(GH):
                    sp.dma_start(q_op[u][h * QD:h * QD + QROWS, c * NB:(c + 1) * NB, h, :].bitcast(F32),
                                 q_dram[bass.ds(n * GH + h, 1), :, c * CH:(c + 1) * CH]
                                 .rearrange("g r t -> (g r) t")).then_inc(q_loaded[u][c], 16)

            def load_k(n, u, c):
                for h in range(GH):
                    sp.dma_start(k_op[u][h * QD:h * QD + KROWS, c * CH:(c + 1) * CH].bitcast(F32),
                                 k_dram[bass.ds(n * GH + h, 1), :, c * CH:(c + 1) * CH]
                                 .rearrange("g r t -> (g r) t")).then_inc(k_loaded[u][c], 16)

            def load_v(n, u):
                sp.dma_start(v_op[u][:, :, :, :].rearrange("p k h r -> p (k h r)"),
                             v_dram[bass.ds(n, 1)].rearrange("g p k r -> (g p) (k r)")).then_inc(v_loaded[u], 16)

            sp.wait_ge(zeros_stored, 16)
            sp.wait_ge(hilo_stored[0], 3 * 16 * CHUNKS)
            sp.wait_ge(hilo_stored[1], 3 * 16 * CHUNKS)
            sp.wait_ge(v_stored, 16 * GROUPS)
            sp.wait_ge(ops_filled, 6)
            for n in range(2):
                for c in range(NC):
                    load_q(n, n, c)
                    load_k(n, n, c)
                load_v(n, n)

            def stage(plan, s, u, small, load=False):
                n = s - 1
                v = 1 - u
                if load:
                    sp.wait_ge(w_split, 1 + n)
                    sp.dma_start(w_raw[:, :], w_all[:, bass.ds(n * PIECE, PIECE)]).then_inc(ld_w, 16)
                for step in plan:
                    if step[0] == "MROWS":
                        _, c, use = step
                        to = u if (c == 0 or plan is PROLOGUE) else v
                        sp.wait_ge(small_read, small + use + 1)
                        for h in range(GH):
                            sp.dma_start(
                                q_op[to][h * QD + KROWS:h * QD + QROWS, c * NB:(c + 1) * NB, h, :].bitcast(F32),
                                max_rows[c][:, h * QD:(h + 1) * QD])\
                                .then_inc(rows_loaded[c], 16)
                    if not load:
                        continue
                    if step == ("END", 0):
                        sp.wait_ge(t_ready, NT * n + SEG_T[0])
                        load_q(s + 1, v, 0)
                    if step == ("T", 1, TI, 0):
                        sp.wait_ge(t_ready, NT * n + SEG_T[0] + TI * GH)
                        load_k(s + 1, v, 0)
                    if step == ("END", NC - 1):
                        sp.wait_ge(t_ready, NT * n + NT)
                        load_q(s + 1, v, 1)
                        load_k(s + 1, v, 1)
                        sp.wait_ge(pv_done, PB + NPV * n + NPV)
                        load_v(s + 1, v)

            stage(PROLOGUE, 0, 0, 0)
            with sp.Fori(0, GROUPS // 2 - 1) as i:
                stage(STEADY, i * 2 + 1, 1, i * (2 * SMALL) + SMALL_0, load=True)
                stage(STEADY, i * 2 + 2, 0, i * (2 * SMALL) + SMALL_0 + SMALL, load=True)
            stage(STEADY, GROUPS - 1, 1, SMALL_0 + (GROUPS - 2) * SMALL)
            stage(LAST, GROUPS, 0, SMALL_0 + (GROUPS - 1) * SMALL)

            with sp.Fori(0, CHUNKS) as ch:
                sp.wait_ge(f_z, ch + 1)
                sp.dma_start(out[bass.ds(ch * CH, CH), :].rearrange("(t p) d -> p t d", p=P), z_sb[:, :, :])\
                    .then_inc(out_stored, 16)
            sp.wait_ge(out_stored, 16 * CHUNKS + 16)

        @block.gpsimd
        def _(pool):
            for credit in (w_split,):
                pool.sem_inc(credit, 1)
            pool.memset(flat[0].bitcast(F32), 0.0).then_inc(ops_filled, 1)
            for n in range(2 * CHUNKS):
                pool.wait_ge(turned, n + 1)
                if n >= 2:
                    pool.wait_ge(lo_ready, n - 1)
                pool.tensor_tensor(roped[:, n % 2, :], by_cos[:, n % 2, :], by_sin[:, n % 2, :], ALU.add)\
                    .then_inc(roped_ready, 1)
            pool.memset(flat[1].bitcast(F32), 0.0).then_inc(ops_filled, 1)
            pool.memset(k_op[0][:, :].bitcast(F32), 1.0).then_inc(ops_filled, 1)
            pool.memset(k_op[1][:, :].bitcast(F32), 1.0).then_inc(ops_filled, 1)
            pool.memset(o_sb[NC - 1][:, :], 1.0).then_inc(ops_filled, 1)
            pool.memset(minus_half[:, :], -0.5).then_inc(ops_filled, 1)

            def stage(plan, n, split=False):
                for step in plan:
                    if step[0] != "T":
                        continue
                    _, c, kt, h = step
                    if kt >= TI * c and h == GH - 1:
                        k = T_UNITS.index((c, kt, h))
                        off = P * (kt - TI * c)
                        pool.wait_ge(t_exped, TB + NT * n + k + 1)
                        pool.sem_inc(pool_turn, 1)
                        tile = num[:, (k // GH) % PB, :, off:off + P]
                        pool.affine_select(out=tile, in_=tile, compare_op=ALU.is_ge, fill=0.0, base=0,
                                           pattern=[[0, GH], [1, P]], channel_multiplier=-1)\
                            .then_inc(masked, 1)
                    if split and (c, kt, h) == (0, TI - 1, GH - 1):
                        pool.wait_ge(w_hi_done, n + 1)
                        pool.tensor_tensor(w_lo[:, bass.ds(n * PIECE, PIECE)], w_raw[:, :],
                                           w_hi[:, bass.ds(n * PIECE, PIECE)].bitcast(F32), ALU.subtract)\
                            .then_inc(w_split, 1)

            with pool.Fori(0, GROUPS // 2 - 1) as i:
                stage(STEADY, i * 2, split=True)
                stage(STEADY, i * 2 + 1, split=True)
            stage(STEADY, GROUPS - 2)
            stage(LAST, GROUPS - 1)

            pool.wait_ge(ops_filled, 6)
            with pool.Fori(0, CHUNKS) as ch:
                pool.wait_ge(c_var, ch + 1)
                pool.tensor_tensor(rstd[:, :], veps[:, :], minus_half[:, :], ALU.pow).then_inc(c_rstd, 1)
            with pool.Fori(0, CHUNKS) as ch:
                pool.wait_ge(f_var, ch + 1)
                pool.tensor_tensor(rstd[:, :], veps[:, :], minus_half[:, :], ALU.pow).then_inc(f_rstd, 1)

        @block.scalar
        def _(act):
            for credit in (c_hi, c_mgs, c_store, o_copied):
                act.sem_inc(credit, 1)
            act.dma_start(x_res[:, :, :], x_tok.rearrange("(t p) d -> p t d", p=P)).then_inc(ld_res, 16)
            act.wait_ge(ld_proj, 48)
            for i in (0, 2):
                pair = wqk[:, i, :].rearrange("p (n two) -> p n two", two=2)
                turn = wqk[:, i + 1, :].rearrange("p (n two) -> p n two", two=2)
                act.activation(turn[:, :, 0], pair[:, :, 1], ACT.Copy, scale=-1.0)
                act.activation(turn[:, :, 1], pair[:, :, 0], ACT.Copy).then_inc(rot_ready, 1)

            for n in range(2 * CHUNKS):
                act.wait_ge(roped_ready, n + 1)
                if n >= 2:
                    act.wait_ge(hilo_stored[n % 2], 3 * 16 * (n // 2))
                act.activation(rope_hi[:, n % 2, :].bitcast(F32R), roped[:, n % 2, :], ACT.Copy)\
                    .then_inc(hi_ready, 1)
                if n % 2 == 1:
                    ch = n // 2
                    b, c = divmod(ch, NC)
                    act.wait_ge(v_proj, ch + 1)
                    act.wait_ge(v_cleared, 2)
                    if c == 0 and b > 0:
                        act.wait_ge(v_stored, 16 * NG * b)
                    act.activation(v_stage[:, c * TI:(c + 1) * TI, :, 0:DH],
                                   bank[4 + ch % 2][:, :].rearrange("p (k h d) -> p k h d", k=TI, h=H), ACT.Copy)\
                        .then_inc(v_copied, 1)
            act.wait_ge(ld_small, 16 * 6)
            act.activation(ident_b[:, :], ident[:, :], ACT.Copy).then_inc(small_cast, 1)
            act.activation(mask_b[:, :], mask_f[:, :], ACT.Copy).then_inc(small_cast, 1)

            act.sem_inc(t_exped, TB)
            act.wait_ge(v_stored, 16 * GROUPS)

            def stage(plan, n, split=False):
                scale = float(DH) ** -0.5
                for step in plan:
                    if split and step == ("T", 0, TI - 1, 0):
                        act.wait_ge(ld_w, (n + 1) * 16)
                        act.activation(w_hi[:, bass.ds(n * PIECE, PIECE)], w_raw[:, :], ACT.Copy)\
                            .then_inc(w_hi_done, 1)
                    if step[0] == "T":
                        _, c, kt, h = step
                        k = T_UNITS.index((c, kt, h))
                        off = P * max(0, kt - TI * c)
                        t = k // GH
                        act.wait_ge(t_ready, NT * n + k + 1)
                        if h == 0:
                            act.wait_ge(pv_done, NPV * n + t + 1)
                        act.activation(num[:, t % PB, h, off:CH], t_bank[k % TB][:, off:CH], ACT.Exp, scale=scale)\
                            .then_inc(t_exped, 1)
                    if step[0] == "OCOPY":
                        c = step[1]
                        act.wait_ge(pv_done, PB + NPV * n + (TI if c == 0 else NPV))
                        act.wait_ge(small_ready, SMALL_0 + SMALL * n + (2 if c == NC - 1 else 0))
                        act.activation(o_sb[c][:, :], o_bank[:, :], ACT.Copy).then_inc(o_copied, 1)

            with act.Fori(0, GROUPS // 2 - 1) as i:
                stage(STEADY, i * 2, split=True)
                stage(STEADY, i * 2 + 1, split=True)
            stage(STEADY, GROUPS - 2)
            stage(LAST, GROUPS - 1)

            with act.Fori(0, B) as b:
                for c in range(NC):
                    ch = b * NC + c
                    act.wait_ge(small_read, SMALL_0 + GROUPS * SMALL)
                    act.wait_ge(c_mgt, 1 + ch)
                    act.activation(mg_w[:, :].rearrange("p (i g r) -> p i g r", i=TI, g=NG),
                                   merged[:, bass.ds(b * NG + 1, NG), c * TI:(c + 1) * TI, :]
                                   .rearrange("p g i r -> p i g r"), ACT.Copy).then_inc(c_mg, 1)
                    act.wait_ge(c_mgt, 1 + ch + 1)
                    act.wait_ge(c_y, 1 + ch)
                    act.activation(mg_t[:, :], bank[0][:, :], ACT.Copy).then_inc(c_mgs, 1)
                    act.wait_ge(c_x1, 1 + ch + 1)
                    act.activation(x1[:, bass.ds(ch * TI, TI), :].rearrange("p i d -> p (i d)"), x1_w[:, :], ACT.Copy)\
                        .then_inc(c_store, 1)
                    act.wait_ge(c_x1t, 1 + ch + 1)
                    act.wait_ge(c_log, 1 + ch)
                    act.wait_ge(c_lo, 1 + ch)
                    act.activation(x1_tw[:, :], bank[2][:, :], ACT.Copy).then_inc(c_x1s, 1)
                    act.activation(x1_hi[:, bass.ds(ch * CH, CH)], bank[2][:, :], ACT.Copy).then_inc(c_hi, 1)
                    act.wait_ge(c_top, 1 + ch + 1)
                    act.wait_ge(c_done, ch * 2 + 1)
                    act.activation(expd[:, :, :], logits[:, :, :], ACT.Exp).then_inc(c_exp, 1)

            act.sem_inc(f_eo, 2)
            with act.Fori(0, CHUNKS) as ch:
                for n in range(FFN_STEPS):
                    if n < UNITS:
                        act.wait_ge(f_ab, ch * UNITS + n + 1)
                        act.wait_ge(f_hid, ch * UNITS + n + 1)
                        act.activation(silu_sb[:, n % 2, :], bank[2 * (n % 2)][:, :], ACT.Silu).then_inc(f_silu, 1)
                    if 1 <= n <= UNITS:
                        m = n - 1
                        act.wait_ge(f_hid, ch * UNITS + m + 1 + 2)
                        act.wait_ge(f_w2, ch * UNITS + m + 1)
                        act.activation(hid_hi[:, m % HB, :], hid[:, m % HB, :], ACT.Copy).then_inc(f_hi, 1)
                    if n >= EO_STEP and (n - EO_STEP) % FT == 0 and n < EO_STEP + UNITS:
                        e = (n - EO_STEP) // FT
                        act.wait_ge(f_w2, ch * UNITS + (FT * (e + 1) + HB))
                        act.wait_ge(f_tr, ch * E + e + 1)
                        act.activation(eo_sb[:, e % 2, :], bank[4 + e % 2][:, :], ACT.Copy).then_inc(f_eo, 1)

        @block.vector
        def _(dve):
            for credit in (c_lo, c_done, c_x1, c_top, f_y):
                dve.sem_inc(credit, 1)
            steps = [0]

            def step_done(ins, looped=None):
                steps[0] += 1
                ins.then_inc(dve_step, 1)
                dve.wait_ge(dve_step, steps[0])

            dve.sem_inc(s_reduced, SB)
            dve.sem_inc(f_hid, 2)
            dve.sem_inc(f_lo, HB)

            dve.memset(v_stage[:, :, :, :], 0.0).then_inc(v_cleared, 1)
            dve.wait_ge(v_cleared, 1)
            dve.memset(v_stage[:, :, :, DH:DH + 1], 1.0).then_inc(v_cleared, 1)
            dve.wait_ge(ld_tab, 32)

            def split_rope(n):
                dve.wait_ge(hi_ready, n + 1)
                if n >= 2:
                    dve.wait_ge(hilo_stored[n % 2], 3 * 16 * (n // 2))
                dve.tensor_tensor(rope_lo[:, n % 2, :].bitcast(F32R), roped[:, n % 2, :], rope_hi[:, n % 2, :],
                                  ALU.subtract).then_inc(lo_ready, 1)

            for n in range(2 * CHUNKS):
                ch = n // 2
                c = ch % NC
                cols = slice(c * CH, (c + 1) * CH)
                dve.wait_ge(proj_ready, n + 1)
                if n >= 2:
                    dve.wait_ge(roped_ready, n - 1)
                dve.tensor_tensor(by_cos[:, n % 2, :], bank[2 * (n % 2)][:, :], cos_sb[:, cols], ALU.mult)
                dve.tensor_tensor(by_sin[:, n % 2, :], bank[2 * (n % 2) + 1][:, :], sin_sb[:, cols], ALU.mult)\
                    .then_inc(turned, 1)
                if n >= 1:
                    split_rope(n - 1)
            split_rope(2 * CHUNKS - 1)
            def split_max(s, c, chain):
                m = CH // QD
                js = slice(c * m, (c + 1) * m)
                top_m = maxima[:, 0, js]
                dve.wait_ge(s_reduced, SB + NS * s + sum(SEG_S[:c + 1]))
                if c > 0:
                    dve.tensor_tensor(top_m, maxima[:, 0, js], maxima[:, 1, js], ALU.max).then_inc(dve_step, 1)
                    dve.wait_ge(dve_step, chain + 1)
                    chain = chain + 1
                dve.tensor_scalar(neg_max[c][:, 0:m].bitcast(F32R), top_m, -1.0, None, ALU.mult).then_inc(dve_step, 1)
                dve.wait_ge(dve_step, chain + 1)
                dve.scalar_tensor_tensor(neg_max[c][:, m:2 * m].bitcast(F32R), top_m, -1.0, neg_max[c][:, 0:m],
                                         ALU.mult, ALU.subtract).then_inc(max_split, 1)

            def stage(plan, s, chain, small):
                done = 0
                for step in plan:
                    if step[0] == "S":
                        _, c, j, half = step
                        k = S_UNITS.index((c, j, half))
                        lo = half * CH
                        width = min(CH, QD * (j + 1) - lo)
                        dve.wait_ge(s_ready, NS * s + k + 1)
                        dve.tensor_reduce(maxima[:, half, j:j + 1], s_bank[k % SB][:, 0:width], AX.X, ALU.max)\
                            .then_inc(s_reduced, 1)
                        done += 1
                        if done == SEG_S[0]:
                            split_max(s, 0, chain)
                            chain = chain + 1
                        if done == NS:
                            split_max(s, 1, chain)
                            chain = chain + 2
                    if step[0] == "MROWS":
                        _, c, use = step
                        dve.wait_ge(small_ready, small + use + 1)
                        dve.tensor_copy(max_rows[c][:, :], small_bank[0:2 * CH // QD, 0:P]).then_inc(small_read, 1)
                    if step[0] == "NORM":
                        _, c, use = step
                        slot = s - 1 if c == NC - 1 and use < SMALL - 1 else s
                        view = small_bank[:, :].rearrange("p (i h r) -> p i h r", i=TI, h=GH)
                        dve.wait_ge(small_ready, small + use + 1)
                        dve.reciprocal(rden[:, :, :], view[:, :, :, DH]).then_inc(dve_step, 1)
                        dve.wait_ge(dve_step, chain + 1)
                        chain = chain + 1
                        dve.tensor_tensor(
                            merged[:, bass.ds(slot, 1), c * TI:(c + 1) * TI, :]
                            .rearrange("p g i (h d) -> p (g i) h d", h=GH),
                            view[:, :, :, 0:DH], rden[:, :, :].unsqueeze(3).broadcast_to([P, TI, GH, DH]),
                            ALU.mult).then_inc(small_read, 1)

            CHAIN_0, CHAIN = 3, 3 + NC
            base = steps[0]
            stage(PROLOGUE, 0, base, 0)
            with dve.Fori(0, GROUPS // 2 - 1) as i:
                for u in range(2):
                    stage(STEADY, i * 2 + (1 + u), i * (2 * CHAIN) + (base + CHAIN_0 + u * CHAIN),
                          i * (2 * SMALL) + (SMALL_0 + u * SMALL))
            stage(STEADY, GROUPS - 1, base + CHAIN_0 + (GROUPS - 2) * CHAIN, SMALL_0 + (GROUPS - 2) * SMALL)
            stage(LAST, GROUPS, base + CHAIN_0 + (GROUPS - 1) * CHAIN, SMALL_0 + (GROUPS - 1) * SMALL)
            steps[0] = base + CHAIN_0 + (GROUPS - 1) * CHAIN + NC + 1

            def layernorm(src, dst, chain, var_sem, rstd_sem, ch, done_sem):
                c0 = chain
                for i in range(TI):
                    dve.bn_stats(stats[:, i, :], src(i)).then_inc(dve_step, 1)
                for i in range(TI):
                    dve.wait_ge(dve_step, c0 + i + 1)
                    dve.sem_inc(dve_turn, 1)
                    dve.bn_aggr(mv[:, i, :], stats[:, i, :]).then_inc(dve_step, 1)
                dve.wait_ge(dve_step, c0 + 2 * TI)
                dve.tensor_scalar(veps[:, :], mv[:, :, 1], EPS, None, ALU.add).then_inc(var_sem, 1)
                dve.wait_ge(rstd_sem, ch + 1)
                for i in range(TI):
                    ins = dve.tensor_scalar(dst(i), src(i), mv[:, i, 0:1], rstd[:, i:i + 1], ALU.subtract, ALU.mult)
                ins.then_inc(done_sem, 1)
                return c0 + 2 * TI

            dve.wait_ge(ld_small, 16 * 6)
            dve.wait_ge(ld_res, 16)
            base = steps[0]
            C_STEPS = 1 + 2 * TI + 11
            with dve.Fori(0, B) as b:
                for c in range(NC):
                    ch = b * NC + c
                    chain = base + ch * C_STEPS

                    def then(ins, k):
                        ins.then_inc(dve_step, 1)
                        dve.wait_ge(dve_step, chain + k)

                    dve.wait_ge(c_y, 1 + ch + 1)
                    then(dve.tensor_tensor(resid[:, :], bank[1][:, :],
                                           x_res[:, bass.ds(ch * TI, TI), :].rearrange("p i d -> p (i d)"), ALU.add), 1)
                    dve.wait_ge(c_x1t, 1 + ch)
                    dve.wait_ge(c_store, 1 + ch)
                    layernorm(lambda i: resid[:, i * D:(i + 1) * D], lambda i: x1_w[:, i * D:(i + 1) * D],
                              chain + 1, c_var, c_rstd, ch, c_x1)
                    k = 1 + 2 * TI
                    dve.wait_ge(c_hi, 1 + ch + 1)
                    dve.tensor_tensor(x1_lo[:, bass.ds(ch * CH, CH)], x1_tw[:, :],
                                      x1_hi[:, bass.ds(ch * CH, CH)].bitcast(F32), ALU.subtract).then_inc(c_lo, 1)
                    dve.wait_ge(c_log, 1 + ch + 1)
                    then(dve.tensor_tensor(logits[:, :, :], bank[3][:, 0:TI * E].rearrange("p (i e) -> p i e", i=TI),
                                           rb[:, :].unsqueeze(1).broadcast_to([P, TI, E]), ALU.add), k + 1)
                    a = logits[:, :, :].unsqueeze(2).broadcast_to([P, TI, E, E])
                    z = logits[:, :, :].unsqueeze(3).broadcast_to([P, TI, E, E])
                    upper = tri[:, 0:1, :].broadcast_to([P, TI, E * E])
                    lower = tri[:, 1:2, :].broadcast_to([P, TI, E * E])
                    gt_f, ge_f = (m[:, :, :, :].rearrange("p i e j -> p i (e j)") for m in (gt, ge))
                    then(dve.tensor_tensor(gt[:, :, :, :], a, z, ALU.is_gt), k + 2)
                    then(dve.tensor_tensor(ge[:, :, :, :], a, z, ALU.is_ge), k + 3)
                    then(dve.tensor_tensor(gt_f, gt_f, upper, ALU.mult), k + 4)
                    then(dve.tensor_tensor(ge_f, ge_f, lower, ALU.mult), k + 5)
                    then(dve.tensor_tensor(gt_f, gt_f, ge_f, ALU.add), k + 6)
                    then(dve.tensor_reduce(rank[:, :, :], gt[:, :, :, :], AX.X, ALU.add), k + 7)
                    then(dve.tensor_reduce(top[:, :], logits[:, :, :], AX.X, ALU.max), k + 8)
                    then(dve.tensor_scalar(chosen[:, :, :], rank[:, :, :], 1.5, None, ALU.is_lt), k + 9)
                    dve.tensor_tensor(logits[:, :, :], logits[:, :, :], top[:, :].unsqueeze(2).broadcast_to([P, TI, E]),
                                      ALU.subtract).then_inc(c_top, 1)
                    dve.wait_ge(c_exp, ch + 1)
                    then(dve.tensor_tensor(expd[:, :, :], expd[:, :, :], chosen[:, :, :], ALU.mult), k + 10)
                    then(dve.tensor_reduce(gsum[:, :], expd[:, :, :], AX.X, ALU.add), k + 11)
                    dve.reciprocal(gsum[:, :], gsum[:, :]).then_inc(c_done, 1)
                    dve.wait_ge(c_done, 1 + 2 * ch + 1)
                    dve.tensor_tensor(gates[:, bass.ds(ch * TI, TI), :], expd[:, :, :],
                                      gsum[:, :].unsqueeze(2).broadcast_to([P, TI, E]), ALU.mult).then_inc(c_done, 1)
                    dve.wait_ge(c_done, 1 + 2 * ch + 2)
            steps[0] = base + CHUNKS * C_STEPS

            base = steps[0]
            F_STEPS = 2 * TI
            with dve.Fori(0, CHUNKS) as ch:
                for n in range(FFN_STEPS):
                    if n < UNITS:
                        dve.wait_ge(f_silu, ch * UNITS + n + 1)
                        dve.wait_ge(f_lo, ch * UNITS + n + 1)
                        dve.tensor_tensor(hid[:, n % HB, :], bank[2 * (n % 2) + 1][:, :], silu_sb[:, n % 2, :],
                                          ALU.mult).then_inc(f_hid, 1)
                    if 1 <= n <= UNITS:
                        m = n - 1
                        dve.wait_ge(f_hi, ch * UNITS + m + 1)
                        dve.wait_ge(f_w2, ch * UNITS + m + 1)
                        dve.tensor_tensor(hid_lo[:, m % HB, :], hid[:, m % HB, :], hid_hi[:, m % HB, :].bitcast(F32),
                                          ALU.subtract).then_inc(f_lo, 1)
                    if n >= Y_STEP and (n - Y_STEP) % FT == 0:
                        e = (n - Y_STEP) // FT
                        dve.wait_ge(f_tr, ch * E + e + 1 + 2)
                        dve.wait_ge(f_y, 1 + ch * E + e)
                        for i in range(TI):
                            before = y_sb[:, i, :] if e else \
                                x1[:, bass.ds(ch * TI + i, 1), :].rearrange("p i d -> p (i d)")
                            ins = dve.scalar_tensor_tensor(
                                y_sb[:, i, :], bank[6][:, i * D:(i + 1) * D],
                                gates[:, bass.ds(ch * TI + i, 1), e:e + 1].rearrange("p i e -> p (i e)"),
                                before, ALU.mult, ALU.add)
                        ins.then_inc(f_y, 1)
                dve.wait_ge(f_y, 1 + ch * E + E)
                dve.wait_ge(out_stored, ch * 16 + 16)
                layernorm(lambda i: y_sb[:, i, :], lambda i: z_sb[:, i, :], ch * F_STEPS + base,
                          f_var, f_rstd, ch, f_z)
                dve.wait_ge(f_z, ch + 1)

        @block.tensor
        def _(pe):
            for credit in (c_mgt, c_y, c_log, c_x1t):
                pe.sem_inc(credit, 1)
            pe.wait_ge(rot_ready, 2)
            for n in range(2 * CHUNKS):
                ch, is_k = divmod(n, 2)
                if n >= 2:
                    pe.wait_ge(turned, n - 1)
                if not is_k:
                    pe.wait_ge(ld_x, 16 * (ch + 1))
                for turn in range(2):
                    ins = pe.matmul(bank[2 * (n % 2) + turn][:, :], wqk[:, 2 * is_k + turn, :],
                                    xT[:, ch * CH:(ch + 1) * CH], start=True, stop=True)
                ins.then_inc(proj_ready, 1)
                if not is_k:
                    if ch >= 2:
                        pe.wait_ge(v_copied, ch - 1)
                    for i in range(TI):
                        ins = pe.matmul(bank[4 + ch % 2][:, i * D:(i + 1) * D],
                                        xT[:, ch * CH + i * P:ch * CH + (i + 1) * P], wv[:, :], start=True, stop=True)
                    ins.then_inc(v_proj, 1)
            pe.wait_ge(turned, 2 * CHUNKS)
            pe.wait_ge(v_copied, CHUNKS)
            pe.wait_ge(ld_small, 16 * 6)
            pe.wait_ge(small_cast, 2)
            pe.sem_inc(pv_done, PB)

            def stage(plan, s, u, turn_u, turn_v, small):
                n = s - 1
                v = 1 - u
                seen = set()

                def once(semaphore, value, key):
                    if key not in seen:
                        seen.add(key)
                        pe.wait_ge(semaphore, value)

                for step in plan:
                    if step[0] == "S":
                        _, c, j, half = step
                        k = S_UNITS.index((c, j, half))
                        once(q_loaded[u][c], turn_u * (16 * GH), ("q", c))
                        once(k_loaded[u][half], turn_u * (16 * GH), ("k", half))
                        lo = half * CH
                        width = min(CH, QD * (j + 1) - lo)
                        diagonal = QD * (j + 1) - lo <= CH
                        pe.wait_ge(s_reduced, NS * s + k + 1)
                        ins = pe.matmul(s_bank[k % SB][:, 0:width], q_op[u][:, j, :, :].rearrange("p h q -> p (h q)"),
                                        k_op[u][:, lo:lo + width], start=True, stop=not diagonal)
                        if diagonal:
                            ins = pe.matmul(s_bank[k % SB][:, width - QD:width], ident_b[:, :], mask_b[:, :],
                                            start=False, stop=True)
                        ins.then_inc(s_ready, 1)
                    if step[0] == "T":
                        _, c, kt, h = step
                        k = T_UNITS.index((c, kt, h))
                        off = P * max(0, kt - TI * c)
                        once(rows_loaded[c], (n + 1) * (16 * GH), ("m", c))
                        pe.wait_ge(t_exped, NT * n + k + 1)
                        pe.matmul(t_bank[k % TB][:, off:CH].rearrange("p (j q) -> p j q", q=QD),
                                  k_op[v][:, kt * P:(kt + 1) * P],
                                  q_op[v][:, c * NB + off // QD:(c + 1) * NB, h, :], start=True, stop=True)\
                            .then_inc(t_ready, 1)
                    if step[0] == "PV":
                        _, c, kt = step
                        t = kt + (TI if c > 0 else 0)
                        off = P * max(0, kt - TI * c)
                        once(v_loaded[v], turn_v * 16, "v")
                        if kt == 0:
                            pe.wait_ge(o_copied, 1 + NC * n + c)
                        pe.wait_ge(t_exped, TB + NT * n + GH * (t + 1))
                        if kt >= TI * c:
                            pe.wait_ge(masked, NC * TI * n + kt + 1)
                        for h in range(GH):
                            ins = pe.matmul(o_bank[h * QD:(h + 1) * QD, off:CH], v_op[v][:, kt, h, :],
                                            num[:, t % PB, h, off:CH], start=kt == 0, stop=kt == TI * (c + 1) - 1,
                                            tile_position=(0, h * QD))
                        ins.then_inc(pv_done, 1)
                    if step[0] == "MROWS":
                        _, c, use = step
                        g = s if (c == 0 or plan is PROLOGUE) else n
                        pe.wait_ge(max_split, NC * g + c + 1)
                        pe.wait_ge(small_read, small + use)
                        pe.transpose(small_bank[0:2 * CH // QD, 0:P], neg_max[c][:, :], ident[:, :])\
                            .then_inc(small_ready, 1)
                    if step[0] == "NORM":
                        _, c, use = step
                        mine = c == 0 or use == SMALL - 1
                        pe.wait_ge(o_copied, 1 + NC * n + ((c + 1) if mine else 0))
                        pe.wait_ge(small_read, small + use)
                        for i in range(TI):
                            ins = pe.transpose(small_bank[:, i * P:(i + 1) * P], o_sb[c][:, i * P:(i + 1) * P],
                                               ident[:, :])
                        ins.then_inc(small_ready, 1)

            stage(PROLOGUE, 0, 0, 1, 0, 0)
            pe.wait_ge(ops_filled, 6)
            with pe.Fori(0, GROUPS // 2 - 1) as i:
                stage(STEADY, i * 2 + 1, 1, i + 1, i + 1, i * (2 * SMALL) + SMALL_0)
                stage(STEADY, i * 2 + 2, 0, i + 2, i + 1, i * (2 * SMALL) + (SMALL_0 + SMALL))
            stage(STEADY, GROUPS - 1, 1, GROUPS // 2, GROUPS // 2, SMALL_0 + (GROUPS - 2) * SMALL)
            stage(LAST, GROUPS, 0, 0, GROUPS // 2, SMALL_0 + (GROUPS - 1) * SMALL)

            pe.wait_ge(small_read, SMALL_0 + GROUPS * SMALL)
            with pe.Fori(0, CHUNKS) as ch:
                pe.wait_ge(c_mg, ch + 1)
                pe.wait_ge(c_mgs, 1 + ch)
                for i in range(TI):
                    ins = pe.transpose(bank[0][:, i * P:(i + 1) * P], mg_w[:, i * P:(i + 1) * P], ident[:, :])
                ins.then_inc(c_mgt, 1)
                pe.wait_ge(c_mgs, 1 + ch + 1)
                pe.wait_ge(c_x1, 1 + ch)
                for i in range(TI):
                    ins = pe.matmul(bank[1][:, i * D:(i + 1) * D], mg_t[:, i * P:(i + 1) * P], wo[:, :],
                                    start=True, stop=True)
                ins.then_inc(c_y, 1)
                pe.wait_ge(c_x1, 1 + ch + 1)
                pe.wait_ge(c_hi, 1 + ch)
                for i in range(TI):
                    ins = pe.transpose(bank[2][:, i * P:(i + 1) * P], x1_w[:, i * P:(i + 1) * P], ident[:, :])
                ins.then_inc(c_x1t, 1)
                pe.wait_ge(c_x1s, ch + 1)
                pe.wait_ge(c_top, 1 + ch)
                for i in range(TI):
                    ins = pe.matmul(bank[3][:, i * E:(i + 1) * E], x1_tw[:, i * P:(i + 1) * P], rw[:, :],
                                    start=True, stop=True)
                ins.then_inc(c_log, 1)

            pe.wait_ge(c_lo, 1 + CHUNKS)
            pe.wait_ge(c_done, 1 + 2 * CHUNKS)
            pe.wait_ge(w_split, 1 + GROUPS - 2)
            pe.sem_inc(f_w2, HB)
            pe.sem_inc(f_tr, 2)
            with pe.Fori(0, CHUNKS) as ch:
                tokens = bass.ds(ch * CH, CH)
                for n in range(FFN_STEPS):
                    if n < UNITS:
                        pe.wait_ge(f_hid, ch * UNITS + n + 1)
                        for w in range(2):
                            at = slice(w * E * F + n * P, w * E * F + (n + 1) * P)
                            for k, (ws, xs) in enumerate(((w_hi, x1_hi), (w_hi, x1_lo), (w_lo, x1_hi))):
                                ins = pe.matmul(bank[2 * (n % 2) + w][:, :], ws[:, at], xs[:, tokens],
                                                start=k == 0, stop=k == 2)
                        ins.then_inc(f_ab, 1)
                    if 2 <= n < UNITS + 2:
                        m = n - 2
                        e, f = divmod(m, FT)
                        if f == 0:
                            pe.wait_ge(f_eo, ch * E + e + 1)
                        pe.wait_ge(f_lo, ch * UNITS + m + 1 + HB)
                        at = slice(2 * E * F + m * P, 2 * E * F + (m + 1) * P)
                        for k, (ws, hs) in enumerate(((w_hi, hid_hi), (w_hi, hid_lo), (w_lo, hid_hi))):
                            ins = pe.matmul(bank[4 + e % 2][:, :], ws[:, at], hs[:, m % HB, :],
                                            start=f == 0 and k == 0, stop=f == FT - 1 and k == 2)
                        ins.then_inc(f_w2, 1)
                    if n >= TR_STEP and (n - TR_STEP) % FT == 0 and n < TR_STEP + UNITS:
                        e = (n - TR_STEP) // FT
                        pe.wait_ge(f_eo, ch * E + e + 1 + 2)
                        pe.wait_ge(f_y, 1 + ch * E + e)
                        for i in range(TI):
                            ins = pe.transpose(bank[6][:, i * P:(i + 1) * P], eo_sb[:, e % 2, i * P:(i + 1) * P],
                                               ident[:, :])
                        ins.then_inc(f_tr, 1)


def kernel(**inputs):
    import concourse.bacc as bacc
    from concourse.bass_utils import run_bass_kernel_spmd

    x = np.ascontiguousarray(inputs["L0_attn_x"])
    tokens = x.reshape(T, D)
    w1 = inputs["L0_ffn_w1"].transpose(1, 0, 2).reshape(D, E * F)
    w3 = inputs["L0_ffn_w3"].transpose(1, 0, 2).reshape(D, E * F)
    w2 = inputs["L0_ffn_w2"].reshape(E * FT, P, D).transpose(1, 0, 2).reshape(P, E * F)
    inv_freq = np.float32(1.0) / np.float32(10000.0) ** (np.arange(0, DH, 2, dtype=np.float32) / np.float32(DH))
    freq = (np.arange(S, dtype=np.float32)[:, None] * inv_freq[None, :]).astype(np.float32)
    row = (np.arange(D) % DH) // 2
    arrays = {
        "x_tok": tokens, "x_feat": np.ascontiguousarray(tokens.T),
        "qw": inputs["L0_attn_qw"], "kw": inputs["L0_attn_kw"], "vw": inputs["L0_attn_vw"], "ow": inputs["L0_attn_ow"],
        "router_w": inputs["L0_ffn_router_w"], "router_b": inputs["L0_ffn_router_b"],
        "w_all": np.concatenate([w1, w3, w2], axis=1),
        "cos_t": np.cos(freq).T[row], "sin_t": np.sin(freq).T[row],
        "ident": np.eye(P, dtype=np.float32),
        "mask": np.where(np.arange(QD)[None, :] > (np.arange(P) % QD)[:, None], np.float32(MASKED), np.float32(0)),
        "tri": np.broadcast_to(np.stack([np.triu(np.ones((E, E), np.float32), 1).ravel(),
                                         np.tril(np.ones((E, E), np.float32), -1).ravel()]), (P, 2, E * E)),
    }
    arrays = {n: np.ascontiguousarray(a) for n, a in arrays.items()}
    nc = bacc.Bacc("TRN2", target_bir_lowering=False, num_devices=1)
    args = [nc.dram_tensor(f"in_{n}", a.shape, mybir.dt.from_np(a.dtype), kind="ExternalInput").ap()
            for n, a in arrays.items()]
    out = nc.dram_tensor("out_tokens", (T, D), F32, kind="ExternalOutput").ap()
    transformer_block(nc, *args, out)
    r = run_bass_kernel_spmd(nc, [{f"in_{n}": a for n, a in arrays.items()}], core_ids=[0])
    return r.results[0]["out_tokens"].reshape(B, S, D)
```

```python
from contextlib import ExitStack

import numpy as np

import concourse.bass as bass
from concourse import mybir

F32 = mybir.dt.float32
F32R = mybir.dt.float32r
BF16 = mybir.dt.bfloat16
ALU = mybir.AluOpType
ACT = mybir.ActivationFunctionType
AX = mybir.AxisListType

P = 128
B, S, D = 2, 1024, 128
H = 16
DH = D // H
E, F = 4, 512
T = B * S
EPS = 1e-5

GH = 4
QD = P // GH
NG = H // GH
GROUPS = B * NG
CH = 512
NC = S // CH
CHUNKS = T // CH
TI = CH // P
NB = CH // QD
KT = S // P
QROWS = 3 * DH + 2
KROWS = 3 * DH
MASKED = -1e30
FT = F // P
UNITS = E * FT

S_UNITS = [(0, j, 0) for j in range(CH // QD)]
S_UNITS += [(1, j, half) for j in range(CH // QD, S // QD) for half in range(2)]
T_UNITS = [(c, kt, h) for c in range(NC) for kt in range(TI * (c + 1)) for h in range(GH)]
NS = len(S_UNITS)
NT = len(T_UNITS)
SEG_S = [sum(u[0] == c for u in S_UNITS) for c in range(NC)]
SEG_T = [sum(u[0] == c for u in T_UNITS) for c in range(NC)]
NPV = NT // GH
SB = 3
TB = 3
HB = 4
PB = 3


C_STEPS = 14
C_FROM, C_EVERY = 6, 3


def stage_plan(with_s, with_t):
    plan = []
    for c in range(NC):
        s_units = [u for u in S_UNITS if u[0] == c] if with_s else []
        t_units = [u for u in T_UNITS if u[0] == c] if with_t else []
        kept = 6 if c == NC - 1 and with_t else 0
        steps = max(SEG_S[c], SEG_T[c])
        done_s = 0
        for x in range(steps):
            if x < len(t_units):
                plan.append(("T", *t_units[x]))
                at = T_UNITS.index(t_units[x]) - C_FROM
                if not with_s and at >= 0 and at % C_EVERY == 0 and at // C_EVERY < C_STEPS:
                    plan.append(("C", at // C_EVERY))
            want = (x + 1) * (len(s_units) - kept) // steps
            while s_units and done_s < want:
                plan.append(("S", *s_units[done_s]))
                done_s += 1
            if with_t and x % GH == GH - 1:
                kt = x // GH
                if kt >= 1:
                    plan.append(("PV", c, kt - 1))
                elif c > 0:
                    plan.append(("PV", c - 1, TI * c - 1))
                    plan.append(("OCOPY", c - 1))
            if x == 5:
                if c > 0 and with_s:
                    plan.append(("MROWS", c - 1))
                if c == 0 and with_t:
                    plan.append(("MROWS", NC - 1))
            if x == 11 and with_t:
                plan.append(("NORM", (c - 1) % NC))
        if c == NC - 1 and with_t:
            while s_units and done_s < len(s_units):
                plan.append(("S", *s_units[done_s]))
                done_s += 1
            plan.append(("PV", c, TI * (c + 1) - 1))
            plan.append(("OCOPY", c))
        plan.append(("END", c))
    if with_t and not with_s:
        plan.append(("NORM", NC - 1))
    uses = iter(range(len(plan)))
    return [(*step, next(uses)) if step[0] in ("MROWS", "NORM") else step for step in plan]


PROLOGUE = stage_plan(True, False)
STEADY = stage_plan(True, True)
LAST = stage_plan(False, True)
SMALL_0 = sum(x[0] in ("MROWS", "NORM") for x in PROLOGUE)
SMALL = sum(x[0] in ("MROWS", "NORM") for x in STEADY)
PIECE = 3 * E * F // (GROUPS - 2)
assert NS % SB == 0 and NT % TB == 0 and NPV % PB == 0


W2_LAG = 3
EO_STEP = TR_STEP = FT + W2_LAG
Y_STEP = TR_STEP + 1
VAR_STEP = Y_STEP + UNITS - FT
RSTD_STEP = VAR_STEP + 1
Z_STEP = VAR_STEP + 3
HEAD = Z_STEP + 1 - UNITS
assert HEAD + C_STEPS <= HEAD + UNITS and Y_STEP + UNITS > Z_STEP


def transformer_block(nc, x_tok, x_feat, qw, kw, vw, ow, router_w, router_b, w_all,
                      cos_t, sin_t, ident_d, mask_d, tri_d, out):
    nc.disable_value_cache = True
    ctx = ExitStack()
    with ctx:
        def sb(name, shape, dt=F32):
            return ctx.enter_context(nc.sbuf_tensor(name, shape, dt))

        def sem(name):
            return ctx.enter_context(nc.semaphore(name))

        bank = [ctx.enter_context(nc.psum_tensor(f"bank{i}", [P, CH], F32)) for i in range(8)]
        s_bank, t_bank, o_bank, small_bank = bank[0:3], bank[3:6], bank[6], bank[7]

        q_dram = nc.dram_tensor("q_scratch", (B * H, QROWS, S), F32).ap()
        k_dram = nc.dram_tensor("k_scratch", (B * H, KROWS, S), F32).ap()
        v_dram = nc.dram_tensor("v_scratch", (GROUPS, P, KT, GH * QD), F32).ap()

        cos_sb, sin_sb = sb("cos_sb", [P, S]), sb("sin_sb", [P, S])
        ident = sb("ident", [P, P])
        mask_f = sb("mask_f", [P, QD])
        ident_b, mask_b = sb("ident_b", [P, P], BF16), sb("mask_b", [P, QD], BF16)
        tri = sb("tri", [P, 2, E * E])
        wqk = sb("wqk", [P, 4, D])
        wv, wo = sb("wv", [P, D]), sb("wo", [P, D])
        rw, rb = sb("rw", [P, E]), sb("rb", [P, E])
        xT = sb("xT", [P, T])
        x_res = sb("x_res", [P, T // P, D])
        w_raw = sb("w_raw", [P, PIECE])
        w_hi, w_lo = sb("w_hi", [P, 3 * E * F], F32R), sb("w_lo", [P, 3 * E * F], F32R)

        by_cos, by_sin = sb("by_cos", [P, 2, CH]), sb("by_sin", [P, 2, CH])
        roped = sb("roped", [P, 2, CH])
        rope_hi, rope_lo = sb("rope_hi", [P, 2, CH]), sb("rope_lo", [P, 2, CH])

        q_op = [sb(f"q_op{u}", [P, S // QD, GH, QD], F32R) for u in range(2)]
        k_op = [sb(f"k_op{u}", [P, S], F32R) for u in range(2)]
        v_op = [sb(f"v_op{u}", [P, KT, GH, QD]) for u in range(2)]
        num = sb("num", [P, PB, GH, CH])
        maxima = sb("maxima", [P, 2, S // QD])
        neg_max = [sb(f"neg_max{c}", [P, 2 * CH // QD]) for c in range(NC)]
        max_rows = [sb(f"max_rows{c}", [2 * CH // QD, P]) for c in range(NC)]
        o_sb = [sb(f"o_sb{c}", [P, CH]) for c in range(NC)]
        rden = sb("rden", [P, TI, GH])
        merged = sb("merged", [P, GROUPS + 1, S // P, QD])
        v_stage = num[:, :, :, :].rearrange("p a b c -> p (a b c)")[:, 0:KT * H * QD]\
            .rearrange("p (k h r) -> p k h r", k=KT, h=H)

        mg_w, mg_t, x1_w, x1_tw = (sb(n, [P, CH]) for n in ("mg_w", "mg_t", "x1_w", "x1_tw"))
        resid = sb("resid", [P, CH])
        x1 = sb("x1", [P, T // P, D])
        flat = [q_op[u][:, :, :, :].rearrange("p j h q -> p (j h q)") for u in range(2)]
        x1_hi, x1_lo = flat[0][:, 0:T], flat[0][:, T:2 * T]
        stats, mv = sb("stats", [P, TI, 6]), sb("mv", [P, TI, 2])
        veps, rstd, minus_half = sb("veps", [P, TI]), sb("rstd", [P, TI]), sb("minus_half", [P, TI])
        logits = sb("logits", [P, TI, E])
        gt, ge = sb("gt", [P, TI, E, E]), sb("ge", [P, TI, E, E])
        rank, chosen = sb("rank", [P, TI, E]), sb("chosen", [P, TI, E])
        top, expd, gsum = sb("top", [P, TI]), sb("expd", [P, TI, E]), sb("gsum", [P, TI])
        gates = sb("gates", [P, T // P, E])
        hid_hi, hid_lo = (flat[1][:, i * HB * CH:(i + 1) * HB * CH].rearrange("p (n t) -> p n t", n=HB)
                          for i in range(2))
        hid, silu_sb, eo_sb = num[:, 0, :, :], num[:, 1, 0:2, :], num[:, 1, 2:4, :]
        y_sb, z_sb = (num[:, 2, i, :].rearrange("p (i d) -> p i d", i=TI) for i in range(2))

        ld_proj, ld_tab, ld_x, ld_res, ld_small = (sem(n) for n in (
            "ld_proj", "ld_tab", "ld_x", "ld_res", "ld_small"))
        ld_w = sem("ld_w")
        zeros_stored = sem("zeros_stored")
        ops_filled = sem("ops_filled")
        q_loaded = [[sem(f"q_loaded{u}{c}") for c in range(NC)] for u in range(2)]
        k_loaded = [[sem(f"k_loaded{u}{c}") for c in range(NC)] for u in range(2)]
        v_loaded = [sem(f"v_loaded{u}") for u in range(2)]
        rot_ready, proj_ready, turned, roped_ready, hi_ready, lo_ready = (sem(n) for n in (
            "rot_ready", "proj_ready", "turned", "roped_ready", "hi_ready", "lo_ready"))
        hilo_stored = [sem(f"hilo_stored{i}") for i in range(2)]
        v_proj, v_cleared, v_copied, v_stored = (sem(n) for n in ("v_proj", "v_cleared", "v_copied", "v_stored"))
        s_ready, s_reduced = sem("s_ready"), sem("s_reduced")
        t_ready, t_exped = sem("t_ready"), sem("t_exped")
        masked, pv_done, o_copied = sem("masked"), sem("pv_done"), sem("o_copied")
        max_split, small_ready, small_read = sem("max_split"), sem("small_ready"), sem("small_read")
        rows_loaded = [sem(f"rows_loaded{c}") for c in range(NC)]
        dve_step, dve_turn, pool_turn = sem("dve_step"), sem("dve_turn"), sem("pool_turn")
        w_split, w_hi_done, small_cast = sem("w_split"), sem("w_hi_done"), sem("small_cast")
        c_mg, c_mgt, c_mgs, c_y, c_var, c_rstd, c_x1, c_x1t, c_hi, c_log, c_lo, c_exp, c_store, c_top = (
            sem(n) for n in ("c_mg", "c_mgt", "c_mgs", "c_y", "c_var", "c_rstd", "c_x1", "c_x1t",
                             "c_hi", "c_log", "c_lo", "c_exp", "c_store", "c_top"))
        c_done = sem("c_done")
        f_ab, f_silu, f_hid, f_hi, f_lo, f_eo, f_tr, f_y = (sem(n) for n in (
            "f_ab", "f_silu", "f_hid", "f_hi", "f_lo", "f_eo", "f_tr", "f_y"))
        f_w2 = sem("f_w2")
        c_step, f_step = sem("c_step"), sem("f_step")
        f_var, f_rstd, f_z = sem("f_var"), sem("f_rstd"), sem("f_z")
        out_stored = sem("out_stored")

        block = ctx.enter_context(nc.Block())

        @block.sync
        def _(sp):
            sp.sem_inc(out_stored, 16)
            for w, i in ((qw, 0), (kw, 2)):
                sp.dma_start(wqk[:, i, :], w).then_inc(ld_proj, 16)
            sp.dma_start(wv[:, :], vw).then_inc(ld_proj, 16)
            for ch in range(CHUNKS):
                sp.dma_start(xT[:, ch * CH:(ch + 1) * CH], x_feat[:, ch * CH:(ch + 1) * CH]).then_inc(ld_x, 16)
                if ch == 0:
                    sp.dma_start(cos_sb[:, :], cos_t).then_inc(ld_tab, 16)
                    sp.dma_start(sin_sb[:, :], sin_t).then_inc(ld_tab, 16)
                sp.wait_ge(ld_x, 16 * (ch + 1))
            for dst, src in ((ident[:, :], ident_d), (mask_f[:, :], mask_d), (wo[:, :], ow), (rw[:, :], router_w),
                             (tri[:, :, :], tri_d), (rb[:, :], router_b.partition_broadcast(P))):
                sp.dma_start(dst, src).then_inc(ld_small, 16)
            sp.wait_ge(ops_filled, 1)
            sp.dma_start(q_dram[:, KROWS:QROWS, :],
                         flat[0][0:B * H * 2, 0:S].bitcast(F32))\
                .then_inc(zeros_stored, 16)
            for n in range(2 * CHUNKS):
                ch, is_k = divmod(n, 2)
                b, c = divmod(ch, NC)
                cols = slice(c * CH, (c + 1) * CH)
                heads = slice(b * H, (b + 1) * H)
                dram = k_dram if is_k else q_dram
                hi_at, lo_at = ((0, 2), 1) if is_k else ((0, 1), 2)
                sp.wait_ge(hi_ready, n + 1)
                for r in hi_at:
                    sp.dma_start(dram[heads, r * DH:(r + 1) * DH, cols],
                                 rope_hi[:, n % 2, :])\
                        .then_inc(hilo_stored[n % 2], 16)
                sp.wait_ge(lo_ready, n + 1)
                sp.dma_start(dram[heads, lo_at * DH:(lo_at + 1) * DH, cols],
                             rope_lo[:, n % 2, :])\
                    .then_inc(hilo_stored[n % 2], 16)
                if is_k and c == NC - 1:
                    sp.wait_ge(v_copied, NC * (b + 1))
                    for g in range(NG):
                        sp.dma_start(v_dram[b * NG + g],
                                     v_stage[:, :, g * GH:(g + 1) * GH, :].rearrange("p k h r -> p k (h r)"))\
                            .then_inc(v_stored, 16)

            def load_q(n, u, c):
                for h in range(GH):
                    sp.dma_start(q_op[u][h * QD:h * QD + QROWS, c * NB:(c + 1) * NB, h, :].bitcast(F32),
                                 q_dram[bass.ds(n * GH + h, 1), :, c * CH:(c + 1) * CH]
                                 .rearrange("g r t -> (g r) t")).then_inc(q_loaded[u][c], 16)

            def load_k(n, u, c):
                for h in range(GH):
                    sp.dma_start(k_op[u][h * QD:h * QD + KROWS, c * CH:(c + 1) * CH].bitcast(F32),
                                 k_dram[bass.ds(n * GH + h, 1), :, c * CH:(c + 1) * CH]
                                 .rearrange("g r t -> (g r) t")).then_inc(k_loaded[u][c], 16)

            def load_v(n, u):
                sp.dma_start(v_op[u][:, :, :, :].rearrange("p k h r -> p (k h r)"),
                             v_dram[bass.ds(n, 1)].rearrange("g p k r -> (g p) (k r)")).then_inc(v_loaded[u], 16)

            sp.wait_ge(zeros_stored, 16)
            sp.wait_ge(hilo_stored[0], 3 * 16 * CHUNKS)
            sp.wait_ge(hilo_stored[1], 3 * 16 * CHUNKS)
            sp.wait_ge(v_stored, 16 * GROUPS)
            sp.wait_ge(ops_filled, 6)
            for n in range(2):
                for c in range(NC):
                    load_q(n, n, c)
                    load_k(n, n, c)
                load_v(n, n)

            def stage(plan, s, u, small, load=False):
                n = s - 1
                v = 1 - u
                if load:
                    sp.wait_ge(w_split, 1 + n)
                    sp.dma_start(w_raw[:, :], w_all[:, bass.ds(n * PIECE, PIECE)]).then_inc(ld_w, 16)
                for step in plan:
                    if step[0] == "MROWS":
                        _, c, use = step
                        to = u if (c == 0 or plan is PROLOGUE) else v
                        sp.wait_ge(small_read, small + use + 1)
                        for h in range(GH):
                            sp.dma_start(
                                q_op[to][h * QD + KROWS:h * QD + QROWS, c * NB:(c + 1) * NB, h, :].bitcast(F32),
                                max_rows[c][:, h * QD:(h + 1) * QD])\
                                .then_inc(rows_loaded[c], 16)
                    if not load:
                        continue
                    if step == ("END", 0):
                        sp.wait_ge(t_ready, NT * n + SEG_T[0])
                        load_q(s + 1, v, 0)
                    if step == ("T", 1, TI, 0):
                        sp.wait_ge(t_ready, NT * n + SEG_T[0] + TI * GH)
                        load_k(s + 1, v, 0)
                    if step == ("END", NC - 1):
                        sp.wait_ge(t_ready, NT * n + NT)
                        load_q(s + 1, v, 1)
                        load_k(s + 1, v, 1)
                        sp.wait_ge(pv_done, PB + NPV * n + NPV)
                        load_v(s + 1, v)

            stage(PROLOGUE, 0, 0, 0)
            with sp.Fori(0, GROUPS // 2 - 1) as i:
                stage(STEADY, i * 2 + 1, 1, i * (2 * SMALL) + SMALL_0, load=True)
                stage(STEADY, i * 2 + 2, 0, i * (2 * SMALL) + SMALL_0 + SMALL, load=True)
            stage(STEADY, GROUPS - 1, 1, SMALL_0 + (GROUPS - 2) * SMALL)
            stage(LAST, GROUPS, 0, SMALL_0 + (GROUPS - 1) * SMALL)

            with sp.Fori(0, CHUNKS) as ch:
                sp.wait_ge(f_z, 1 + ch + 1)
                sp.dma_start(out[bass.ds(ch * CH, CH), :].rearrange("(t p) d -> p t d", p=P), z_sb[:, :, :])\
                    .then_inc(out_stored, 16)
            sp.wait_ge(out_stored, 16 * CHUNKS + 16)

        @block.gpsimd
        def _(pool):
            for credit in (w_split,):
                pool.sem_inc(credit, 1)
            pool.memset(flat[0].bitcast(F32), 0.0).then_inc(ops_filled, 1)
            for n in range(2 * CHUNKS):
                pool.wait_ge(turned, n + 1)
                if n >= 2:
                    pool.wait_ge(lo_ready, n - 1)
                pool.tensor_tensor(roped[:, n % 2, :], by_cos[:, n % 2, :], by_sin[:, n % 2, :], ALU.add)\
                    .then_inc(roped_ready, 1)
            pool.memset(flat[1].bitcast(F32), 0.0).then_inc(ops_filled, 1)
            pool.memset(k_op[0][:, :].bitcast(F32), 1.0).then_inc(ops_filled, 1)
            pool.memset(k_op[1][:, :].bitcast(F32), 1.0).then_inc(ops_filled, 1)
            pool.memset(o_sb[NC - 1][:, :], 1.0).then_inc(ops_filled, 1)
            pool.memset(minus_half[:, :], -0.5).then_inc(ops_filled, 1)

            def stage(plan, n, split=False):
                for step in plan:
                    if step[0] == "C":
                        between(0, step[1], first=True)
                    if step[0] != "T":
                        continue
                    _, c, kt, h = step
                    if kt >= TI * c and h == GH - 1:
                        k = T_UNITS.index((c, kt, h))
                        off = P * (kt - TI * c)
                        pool.wait_ge(t_exped, TB + NT * n + k + 1)
                        pool.sem_inc(pool_turn, 1)
                        tile = num[:, (k // GH) % PB, :, off:off + P]
                        pool.affine_select(out=tile, in_=tile, compare_op=ALU.is_ge, fill=0.0, base=0,
                                           pattern=[[0, GH], [1, P]], channel_multiplier=-1)\
                            .then_inc(masked, 1)
                    if split and (c, kt, h) == (0, TI - 1, GH - 1):
                        pool.wait_ge(w_hi_done, n + 1)
                        pool.tensor_tensor(w_lo[:, bass.ds(n * PIECE, PIECE)], w_raw[:, :],
                                           w_hi[:, bass.ds(n * PIECE, PIECE)].bitcast(F32), ALU.subtract)\
                            .then_inc(w_split, 1)

            with pool.Fori(0, GROUPS // 2 - 1) as i:
                stage(STEADY, i * 2, split=True)
                stage(STEADY, i * 2 + 1, split=True)
            stage(STEADY, GROUPS - 2)

            def between(ch, r, first=False):
                if r == 3:
                    pool.wait_ge(c_var, ch + 1)
                    pool.tensor_tensor(rstd[:, :], veps[:, :], minus_half[:, :], ALU.pow).then_inc(c_rstd, 1)

            def experts(ch, n):
                if 1 <= n <= UNITS:
                    m = n - 1
                    pool.wait_ge(f_hi, ch * UNITS + m + 1)
                    pool.wait_ge(f_w2, ch * UNITS + m + 1)
                    pool.tensor_tensor(hid_lo[:, m % HB, :], hid[:, m % HB, :], hid_hi[:, m % HB, :].bitcast(F32),
                                       ALU.subtract).then_inc(f_lo, 1)
                if n == RSTD_STEP:
                    pool.wait_ge(f_var, ch + 1)
                    pool.tensor_tensor(rstd[:, :], veps[:, :], minus_half[:, :], ALU.pow).then_inc(f_rstd, 1)

            pool.wait_ge(ops_filled, 6)
            stage(LAST, GROUPS - 1)
            for n in range(HEAD):
                experts(0, n)
            with pool.Fori(0, CHUNKS - 1) as i:
                for n in range(HEAD, HEAD + UNITS):
                    experts(i, n)
                    if n >= UNITS:
                        experts(i + 1, n - UNITS)
                    between(i + 1, n - HEAD)
            for n in range(HEAD, Z_STEP + 1):
                experts(CHUNKS - 1, n)

        @block.scalar
        def _(act):
            for credit in (c_hi, c_mgs, c_store, o_copied):
                act.sem_inc(credit, 1)
            act.dma_start(x_res[:, :, :], x_tok.rearrange("(t p) d -> p t d", p=P)).then_inc(ld_res, 16)
            act.wait_ge(ld_proj, 48)
            for i in (0, 2):
                pair = wqk[:, i, :].rearrange("p (n two) -> p n two", two=2)
                turn = wqk[:, i + 1, :].rearrange("p (n two) -> p n two", two=2)
                act.activation(turn[:, :, 0], pair[:, :, 1], ACT.Copy, scale=-1.0)
                act.activation(turn[:, :, 1], pair[:, :, 0], ACT.Copy).then_inc(rot_ready, 1)

            for n in range(2 * CHUNKS):
                act.wait_ge(roped_ready, n + 1)
                if n >= 2:
                    act.wait_ge(hilo_stored[n % 2], 3 * 16 * (n // 2))
                act.activation(rope_hi[:, n % 2, :].bitcast(F32R), roped[:, n % 2, :], ACT.Copy)\
                    .then_inc(hi_ready, 1)
                if n % 2 == 1:
                    ch = n // 2
                    b, c = divmod(ch, NC)
                    act.wait_ge(v_proj, ch + 1)
                    act.wait_ge(v_cleared, 2)
                    if c == 0 and b > 0:
                        act.wait_ge(v_stored, 16 * NG * b)
                    act.activation(v_stage[:, c * TI:(c + 1) * TI, :, 0:DH],
                                   bank[4 + ch % 2][:, :].rearrange("p (k h d) -> p k h d", k=TI, h=H), ACT.Copy)\
                        .then_inc(v_copied, 1)
            act.wait_ge(ld_small, 16 * 6)
            act.activation(ident_b[:, :], ident[:, :], ACT.Copy).then_inc(small_cast, 1)
            act.activation(mask_b[:, :], mask_f[:, :], ACT.Copy).then_inc(small_cast, 1)

            act.sem_inc(t_exped, TB)
            act.wait_ge(v_stored, 16 * GROUPS)

            def stage(plan, n, split=False):
                scale = float(DH) ** -0.5
                for step in plan:
                    if split and step == ("T", 0, TI - 1, 0):
                        act.wait_ge(ld_w, (n + 1) * 16)
                        act.activation(w_hi[:, bass.ds(n * PIECE, PIECE)], w_raw[:, :], ACT.Copy)\
                            .then_inc(w_hi_done, 1)
                    if step[0] == "T":
                        _, c, kt, h = step
                        k = T_UNITS.index((c, kt, h))
                        off = P * max(0, kt - TI * c)
                        t = k // GH
                        act.wait_ge(t_ready, NT * n + k + 1)
                        if h == 0:
                            act.wait_ge(pv_done, NPV * n + t + 1)
                        act.activation(num[:, t % PB, h, off:CH], t_bank[k % TB][:, off:CH], ACT.Exp, scale=scale)\
                            .then_inc(t_exped, 1)
                    if step[0] == "OCOPY":
                        c = step[1]
                        act.wait_ge(pv_done, PB + NPV * n + (TI if c == 0 else NPV))
                        act.wait_ge(small_ready, SMALL_0 + SMALL * n + (2 if c == NC - 1 else 0))
                        act.activation(o_sb[c][:, :], o_bank[:, :], ACT.Copy).then_inc(o_copied, 1)
                    if step[0] == "C":
                        between(0, 0, 0, step[1], first=True)

            with act.Fori(0, GROUPS // 2 - 1) as i:
                stage(STEADY, i * 2, split=True)
                stage(STEADY, i * 2 + 1, split=True)
            stage(STEADY, GROUPS - 2)

            def between(ch, b, c, r, first=False):
                turns = bank[0] if first else bank[7]
                if r == 0:
                    act.wait_ge(small_read, SMALL_0 + (GROUPS - first) * SMALL)
                    act.wait_ge(c_mgt, 1 + ch)
                    act.activation(mg_w[:, :].rearrange("p (i g r) -> p i g r", i=TI, g=NG),
                                   merged[:, bass.ds(b * NG + 1, NG), bass.ds(c * TI, TI), :]
                                   .rearrange("p g i r -> p i g r"), ACT.Copy).then_inc(c_mg, 1)
                if r == 2:
                    act.wait_ge(c_mgt, 1 + ch + 1)
                    act.wait_ge(c_y, 1 + ch)
                    act.activation(mg_t[:, :], turns[:, :], ACT.Copy).then_inc(c_mgs, 1)
                if r == 6:
                    act.wait_ge(c_x1t, 1 + ch + 1)
                    act.wait_ge(c_log, 1 + ch)
                    act.wait_ge(c_lo, 1 + ch)
                    act.activation(x1_hi[:, bass.ds(ch * CH, CH)], turns[:, :], ACT.Copy)
                    act.activation(x1_tw[:, :], turns[:, :], ACT.Copy).then_inc(c_hi, 1)
                    act.wait_ge(c_x1, 1 + ch + 1)
                    act.activation(x1[:, bass.ds(ch * TI, TI), :].rearrange("p i d -> p (i d)"), x1_w[:, :], ACT.Copy)\
                        .then_inc(c_store, 1)
                if r == 11:
                    act.wait_ge(c_top, 1 + ch + 1)
                    act.wait_ge(c_done, ch * 2 + 1)
                    act.activation(expd[:, :, :], logits[:, :, :], ACT.Exp).then_inc(c_exp, 1)

            def experts_hi(ch, n):
                if 1 <= n <= UNITS:
                    m = n - 1
                    act.wait_ge(f_hid, ch * UNITS + m + 1 + 2)
                    act.wait_ge(f_w2, ch * UNITS + m + 1)
                    act.activation(hid_hi[:, m % HB, :], hid[:, m % HB, :], ACT.Copy).then_inc(f_hi, 1)
                if n >= EO_STEP and (n - EO_STEP) % FT == 0 and n < EO_STEP + UNITS:
                    e = (n - EO_STEP) // FT
                    act.wait_ge(f_w2, ch * UNITS + (FT * (e + 1) + HB))
                    act.wait_ge(f_tr, ch * E + e + 1)
                    act.activation(eo_sb[:, e % 2, :], bank[4 + e % 2][:, :], ACT.Copy).then_inc(f_eo, 1)

            def experts_silu(ch, n):
                if n < UNITS:
                    act.wait_ge(f_ab, ch * UNITS + n + 1)
                    act.wait_ge(f_hid, ch * UNITS + n + 1)
                    act.activation(silu_sb[:, n % 2, :], bank[2 * (n % 2)][:, :], ACT.Silu).then_inc(f_silu, 1)

            stage(LAST, GROUPS - 1)
            act.sem_inc(f_eo, 2)
            for n in range(HEAD):
                experts_hi(0, n)
                experts_silu(0, n)
            with act.Fori(0, CHUNKS - 1) as i:
                for n in range(HEAD, HEAD + UNITS):
                    experts_hi(i, n)
                    if n >= UNITS:
                        experts_hi(i + 1, n - UNITS)
                    between(i + 1, (i + 1) // NC, (i + 1) % NC, n - HEAD)
                    experts_silu(i, n)
                    if n >= UNITS:
                        experts_silu(i + 1, n - UNITS)
            for n in range(HEAD, Z_STEP + 1):
                experts_hi(CHUNKS - 1, n)
                experts_silu(CHUNKS - 1, n)

        @block.vector
        def _(dve):
            for credit in (c_lo, c_done, c_x1, c_top, f_y, f_z):
                dve.sem_inc(credit, 1)
            steps = [0]

            def step_done(ins, looped=None):
                steps[0] += 1
                ins.then_inc(dve_step, 1)
                dve.wait_ge(dve_step, steps[0])

            dve.sem_inc(s_reduced, SB)
            dve.sem_inc(f_hid, 2)
            dve.sem_inc(f_lo, HB)

            dve.memset(v_stage[:, :, :, :], 0.0).then_inc(v_cleared, 1)
            dve.wait_ge(v_cleared, 1)
            dve.memset(v_stage[:, :, :, DH:DH + 1], 1.0).then_inc(v_cleared, 1)
            dve.wait_ge(ld_tab, 32)

            def split_rope(n):
                dve.wait_ge(hi_ready, n + 1)
                if n >= 2:
                    dve.wait_ge(hilo_stored[n % 2], 3 * 16 * (n // 2))
                dve.tensor_tensor(rope_lo[:, n % 2, :].bitcast(F32R), roped[:, n % 2, :], rope_hi[:, n % 2, :],
                                  ALU.subtract).then_inc(lo_ready, 1)

            for n in range(2 * CHUNKS):
                ch = n // 2
                c = ch % NC
                cols = slice(c * CH, (c + 1) * CH)
                dve.wait_ge(proj_ready, n + 1)
                if n >= 2:
                    dve.wait_ge(roped_ready, n - 1)
                dve.tensor_tensor(by_cos[:, n % 2, :], bank[2 * (n % 2)][:, :], cos_sb[:, cols], ALU.mult)
                dve.tensor_tensor(by_sin[:, n % 2, :], bank[2 * (n % 2) + 1][:, :], sin_sb[:, cols], ALU.mult)\
                    .then_inc(turned, 1)
                if n >= 1:
                    split_rope(n - 1)
            split_rope(2 * CHUNKS - 1)
            def split_max(s, c, chain):
                m = CH // QD
                js = slice(c * m, (c + 1) * m)
                top_m = maxima[:, 0, js]
                dve.wait_ge(s_reduced, SB + NS * s + sum(SEG_S[:c + 1]))
                if c > 0:
                    dve.tensor_tensor(top_m, maxima[:, 0, js], maxima[:, 1, js], ALU.max).then_inc(dve_step, 1)
                    dve.wait_ge(dve_step, chain + 1)
                    chain = chain + 1
                dve.tensor_scalar(neg_max[c][:, 0:m].bitcast(F32R), top_m, -1.0, None, ALU.mult).then_inc(dve_step, 1)
                dve.wait_ge(dve_step, chain + 1)
                dve.scalar_tensor_tensor(neg_max[c][:, m:2 * m].bitcast(F32R), top_m, -1.0, neg_max[c][:, 0:m],
                                         ALU.mult, ALU.subtract).then_inc(max_split, 1)

            def stage(plan, s, chain, small):
                done = 0
                for step in plan:
                    if step[0] == "S":
                        _, c, j, half = step
                        k = S_UNITS.index((c, j, half))
                        lo = half * CH
                        width = min(CH, QD * (j + 1) - lo)
                        dve.wait_ge(s_ready, NS * s + k + 1)
                        dve.tensor_reduce(maxima[:, half, j:j + 1], s_bank[k % SB][:, 0:width], AX.X, ALU.max)\
                            .then_inc(s_reduced, 1)
                        done += 1
                        if done == SEG_S[0]:
                            split_max(s, 0, chain)
                            chain = chain + 1
                        if done == NS:
                            split_max(s, 1, chain)
                            chain = chain + 2
                    if step[0] == "MROWS":
                        _, c, use = step
                        dve.wait_ge(small_ready, small + use + 1)
                        dve.tensor_copy(max_rows[c][:, :], small_bank[0:2 * CH // QD, 0:P]).then_inc(small_read, 1)
                    if step[0] == "NORM":
                        _, c, use = step
                        slot = s - 1 if c == NC - 1 and use < SMALL - 1 else s
                        view = small_bank[:, :].rearrange("p (i h r) -> p i h r", i=TI, h=GH)
                        dve.wait_ge(small_ready, small + use + 1)
                        dve.reciprocal(rden[:, :, :], view[:, :, :, DH]).then_inc(dve_step, 1)
                        dve.wait_ge(dve_step, chain + 1)
                        chain = chain + 1
                        dve.tensor_tensor(
                            merged[:, bass.ds(slot, 1), c * TI:(c + 1) * TI, :]
                            .rearrange("p g i (h d) -> p (g i) h d", h=GH),
                            view[:, :, :, 0:DH], rden[:, :, :].unsqueeze(3).broadcast_to([P, TI, GH, DH]),
                            ALU.mult).then_inc(small_read, 1)
                    if step[0] == "C":
                        between(0, step[1], first=True)

            CHAIN_0, CHAIN = 3, 3 + NC
            base = steps[0]
            stage(PROLOGUE, 0, base, 0)
            with dve.Fori(0, GROUPS // 2 - 1) as i:
                for u in range(2):
                    stage(STEADY, i * 2 + (1 + u), i * (2 * CHAIN) + (base + CHAIN_0 + u * CHAIN),
                          i * (2 * SMALL) + (SMALL_0 + u * SMALL))
            stage(STEADY, GROUPS - 1, base + CHAIN_0 + (GROUPS - 2) * CHAIN, SMALL_0 + (GROUPS - 2) * SMALL)
            last_base = base + CHAIN_0 + (GROUPS - 1) * CHAIN

            def variance(src, step_sem, chain, var_sem):
                for i in range(TI):
                    dve.bn_stats(stats[:, i, :], src(i)).then_inc(step_sem, 1)
                for i in range(TI):
                    dve.wait_ge(step_sem, chain + (i + 1))
                    dve.sem_inc(dve_turn, 1)
                    dve.bn_aggr(mv[:, i, :], stats[:, i, :]).then_inc(step_sem, 1)
                dve.wait_ge(step_sem, chain + 2 * TI)
                dve.tensor_scalar(veps[:, :], mv[:, :, 1], EPS, None, ALU.add).then_inc(var_sem, 1)

            def normalise(src, dst, done_sem):
                for i in range(TI):
                    ins = dve.tensor_scalar(dst(i), src(i), mv[:, i, 0:1], rstd[:, i:i + 1], ALU.subtract, ALU.mult)
                ins.then_inc(done_sem, 1)

            def between(ch, r, first=False):
                C_CHAIN = 1 + 2 * TI + 11
                turns = bank[0] if first else bank[7]

                def then(ins, k):
                    ins.then_inc(c_step, 1)
                    dve.wait_ge(c_step, ch * C_CHAIN + k)

                k = 1 + 2 * TI
                if r == 2:
                    dve.wait_ge(c_y, 1 + ch + 1)
                    then(dve.tensor_tensor(resid[:, :], turns[:, :],
                                           x_res[:, bass.ds(ch * TI, TI), :].rearrange("p i d -> p (i d)"), ALU.add), 1)
                    variance(lambda i: resid[:, i * D:(i + 1) * D], c_step, ch * C_CHAIN + 1, c_var)
                if r == 5:
                    dve.wait_ge(c_x1t, 1 + ch)
                    dve.wait_ge(c_store, 1 + ch)
                    dve.wait_ge(c_rstd, ch + 1)
                    normalise(lambda i: resid[:, i * D:(i + 1) * D], lambda i: x1_w[:, i * D:(i + 1) * D], c_x1)
                if r == 6:
                    dve.wait_ge(c_hi, 1 + ch + 1)
                    dve.tensor_tensor(x1_lo[:, bass.ds(ch * CH, CH)], x1_tw[:, :],
                                      x1_hi[:, bass.ds(ch * CH, CH)].bitcast(F32), ALU.subtract).then_inc(c_lo, 1)
                a = logits[:, :, :].unsqueeze(2).broadcast_to([P, TI, E, E])
                z = logits[:, :, :].unsqueeze(3).broadcast_to([P, TI, E, E])
                upper = tri[:, 0:1, :].broadcast_to([P, TI, E * E])
                lower = tri[:, 1:2, :].broadcast_to([P, TI, E * E])
                gt_f, ge_f = (m[:, :, :, :].rearrange("p i e j -> p i (e j)") for m in (gt, ge))
                if r == 9:
                    dve.wait_ge(c_log, 1 + ch + 1)
                    then(dve.tensor_tensor(logits[:, :, :], turns[:, 0:TI * E].rearrange("p (i e) -> p i e", i=TI),
                                           rb[:, :].unsqueeze(1).broadcast_to([P, TI, E]), ALU.add), k + 1)
                    then(dve.tensor_tensor(gt[:, :, :, :], a, z, ALU.is_gt), k + 2)
                    then(dve.tensor_tensor(ge[:, :, :, :], a, z, ALU.is_ge), k + 3)
                    then(dve.tensor_tensor(gt_f, gt_f, upper, ALU.mult), k + 4)
                if r == 10:
                    then(dve.tensor_tensor(ge_f, ge_f, lower, ALU.mult), k + 5)
                    then(dve.tensor_tensor(gt_f, gt_f, ge_f, ALU.add), k + 6)
                    then(dve.tensor_reduce(rank[:, :, :], gt[:, :, :, :], AX.X, ALU.add), k + 7)
                    then(dve.tensor_reduce(top[:, :], logits[:, :, :], AX.X, ALU.max), k + 8)
                    then(dve.tensor_scalar(chosen[:, :, :], rank[:, :, :], 1.5, None, ALU.is_lt), k + 9)
                    dve.tensor_tensor(logits[:, :, :], logits[:, :, :], top[:, :].unsqueeze(2).broadcast_to([P, TI, E]),
                                      ALU.subtract).then_inc(c_top, 1)
                if r == C_STEPS - 1:
                    dve.wait_ge(c_exp, ch + 1)
                    then(dve.tensor_tensor(expd[:, :, :], expd[:, :, :], chosen[:, :, :], ALU.mult), k + 10)
                    then(dve.tensor_reduce(gsum[:, :], expd[:, :, :], AX.X, ALU.add), k + 11)
                    dve.reciprocal(gsum[:, :], gsum[:, :]).then_inc(c_done, 1)
                    dve.wait_ge(c_done, 1 + 2 * ch + 1)
                    dve.tensor_tensor(gates[:, bass.ds(ch * TI, TI), :], expd[:, :, :],
                                      gsum[:, :].unsqueeze(2).broadcast_to([P, TI, E]), ALU.mult).then_inc(c_done, 1)
                    dve.wait_ge(c_done, 1 + 2 * ch + 2)

            def experts(ch, n):
                if n < UNITS:
                    dve.wait_ge(f_silu, ch * UNITS + n + 1)
                    dve.wait_ge(f_lo, ch * UNITS + n + 1)
                    dve.tensor_tensor(hid[:, n % HB, :], bank[2 * (n % 2) + 1][:, :], silu_sb[:, n % 2, :],
                                      ALU.mult).then_inc(f_hid, 1)
                if n >= Y_STEP and (n - Y_STEP) % FT == 0 and n < Y_STEP + UNITS:
                    e = (n - Y_STEP) // FT
                    dve.wait_ge(f_tr, ch * E + e + 1 + 2)
                    dve.wait_ge(f_y, 1 + ch * E + e)
                    if e == 0:
                        dve.wait_ge(f_z, ch + 1)
                        dve.wait_ge(c_store, 1 + ch + 1)
                    for i in range(TI):
                        before = y_sb[:, i, :] if e else \
                            x1[:, bass.ds(ch * TI + i, 1), :].rearrange("p i d -> p (i d)")
                        ins = dve.scalar_tensor_tensor(
                            y_sb[:, i, :], bank[6][:, i * D:(i + 1) * D],
                            gates[:, bass.ds(ch * TI + i, 1), e:e + 1].rearrange("p i e -> p (i e)"),
                            before, ALU.mult, ALU.add)
                    ins.then_inc(f_y, 1)
                if n == VAR_STEP:
                    dve.wait_ge(f_y, 1 + ch * E + E)
                    variance(lambda i: y_sb[:, i, :], f_step, ch * (2 * TI), f_var)
                if n == Z_STEP:
                    dve.wait_ge(out_stored, ch * 16 + 16)
                    dve.wait_ge(f_rstd, ch + 1)
                    normalise(lambda i: y_sb[:, i, :], lambda i: z_sb[:, i, :], f_z)

            dve.wait_ge(ld_small, 16 * 6)
            dve.wait_ge(ld_res, 16)
            stage(LAST, GROUPS, last_base, SMALL_0 + (GROUPS - 1) * SMALL)
            for n in range(HEAD):
                experts(0, n)
            with dve.Fori(0, CHUNKS - 1) as i:
                for n in range(HEAD, HEAD + UNITS):
                    if n >= UNITS:
                        experts(i + 1, n - UNITS)
                    experts(i, n)
                    between(i + 1, n - HEAD)
            for n in range(HEAD, Z_STEP + 1):
                experts(CHUNKS - 1, n)

        @block.tensor
        def _(pe):
            for credit in (c_mgt, c_y, c_log, c_x1t):
                pe.sem_inc(credit, 1)
            pe.wait_ge(rot_ready, 2)
            for n in range(2 * CHUNKS):
                ch, is_k = divmod(n, 2)
                if n >= 2:
                    pe.wait_ge(turned, n - 1)
                if not is_k:
                    pe.wait_ge(ld_x, 16 * (ch + 1))
                for turn in range(2):
                    ins = pe.matmul(bank[2 * (n % 2) + turn][:, :], wqk[:, 2 * is_k + turn, :],
                                    xT[:, ch * CH:(ch + 1) * CH], start=True, stop=True)
                ins.then_inc(proj_ready, 1)
                if not is_k:
                    if ch >= 2:
                        pe.wait_ge(v_copied, ch - 1)
                    for i in range(TI):
                        ins = pe.matmul(bank[4 + ch % 2][:, i * D:(i + 1) * D],
                                        xT[:, ch * CH + i * P:ch * CH + (i + 1) * P], wv[:, :], start=True, stop=True)
                    ins.then_inc(v_proj, 1)
            pe.wait_ge(turned, 2 * CHUNKS)
            pe.wait_ge(v_copied, CHUNKS)
            pe.wait_ge(ld_small, 16 * 6)
            pe.wait_ge(small_cast, 2)
            pe.sem_inc(pv_done, PB)

            def stage(plan, s, u, turn_u, turn_v, small):
                n = s - 1
                v = 1 - u
                seen = set()

                def once(semaphore, value, key):
                    if key not in seen:
                        seen.add(key)
                        pe.wait_ge(semaphore, value)

                for step in plan:
                    if step[0] == "S":
                        _, c, j, half = step
                        k = S_UNITS.index((c, j, half))
                        once(q_loaded[u][c], turn_u * (16 * GH), ("q", c))
                        once(k_loaded[u][half], turn_u * (16 * GH), ("k", half))
                        lo = half * CH
                        width = min(CH, QD * (j + 1) - lo)
                        diagonal = QD * (j + 1) - lo <= CH
                        pe.wait_ge(s_reduced, NS * s + k + 1)
                        ins = pe.matmul(s_bank[k % SB][:, 0:width], q_op[u][:, j, :, :].rearrange("p h q -> p (h q)"),
                                        k_op[u][:, lo:lo + width], start=True, stop=not diagonal)
                        if diagonal:
                            ins = pe.matmul(s_bank[k % SB][:, width - QD:width], ident_b[:, :], mask_b[:, :],
                                            start=False, stop=True)
                        ins.then_inc(s_ready, 1)
                    if step[0] == "T":
                        _, c, kt, h = step
                        k = T_UNITS.index((c, kt, h))
                        off = P * max(0, kt - TI * c)
                        once(rows_loaded[c], (n + 1) * (16 * GH), ("m", c))
                        pe.wait_ge(t_exped, NT * n + k + 1)
                        pe.matmul(t_bank[k % TB][:, off:CH].rearrange("p (j q) -> p j q", q=QD),
                                  k_op[v][:, kt * P:(kt + 1) * P],
                                  q_op[v][:, c * NB + off // QD:(c + 1) * NB, h, :], start=True, stop=True)\
                            .then_inc(t_ready, 1)
                    if step[0] == "PV":
                        _, c, kt = step
                        t = kt + (TI if c > 0 else 0)
                        off = P * max(0, kt - TI * c)
                        once(v_loaded[v], turn_v * 16, "v")
                        if kt == 0:
                            pe.wait_ge(o_copied, 1 + NC * n + c)
                        pe.wait_ge(t_exped, TB + NT * n + GH * (t + 1))
                        if kt >= TI * c:
                            pe.wait_ge(masked, NC * TI * n + kt + 1)
                        for h in range(GH):
                            ins = pe.matmul(o_bank[h * QD:(h + 1) * QD, off:CH], v_op[v][:, kt, h, :],
                                            num[:, t % PB, h, off:CH], start=kt == 0, stop=kt == TI * (c + 1) - 1,
                                            tile_position=(0, h * QD))
                        ins.then_inc(pv_done, 1)
                    if step[0] == "MROWS":
                        _, c, use = step
                        g = s if (c == 0 or plan is PROLOGUE) else n
                        pe.wait_ge(max_split, NC * g + c + 1)
                        pe.wait_ge(small_read, small + use)
                        pe.transpose(small_bank[0:2 * CH // QD, 0:P], neg_max[c][:, :], ident[:, :])\
                            .then_inc(small_ready, 1)
                    if step[0] == "NORM":
                        _, c, use = step
                        mine = c == 0 or use == SMALL - 1
                        pe.wait_ge(o_copied, 1 + NC * n + ((c + 1) if mine else 0))
                        pe.wait_ge(small_read, small + use)
                        for i in range(TI):
                            ins = pe.transpose(small_bank[:, i * P:(i + 1) * P], o_sb[c][:, i * P:(i + 1) * P],
                                               ident[:, :])
                        ins.then_inc(small_ready, 1)
                    if step[0] == "C":
                        between(0, step[1], first=True)

            stage(PROLOGUE, 0, 0, 1, 0, 0)
            pe.wait_ge(ops_filled, 6)
            with pe.Fori(0, GROUPS // 2 - 1) as i:
                stage(STEADY, i * 2 + 1, 1, i + 1, i + 1, i * (2 * SMALL) + SMALL_0)
                stage(STEADY, i * 2 + 2, 0, i + 2, i + 1, i * (2 * SMALL) + (SMALL_0 + SMALL))
            stage(STEADY, GROUPS - 1, 1, GROUPS // 2, GROUPS // 2, SMALL_0 + (GROUPS - 2) * SMALL)

            def between(ch, r, first=False):
                turns = bank[0] if first else bank[7]
                if r == 1:
                    pe.wait_ge(c_mg, ch + 1)
                    pe.wait_ge(c_top, 1 + ch)
                    for i in range(TI):
                        ins = pe.transpose(turns[:, i * P:(i + 1) * P], mg_w[:, i * P:(i + 1) * P], ident[:, :])
                    ins.then_inc(c_mgt, 1)
                if r == 2:
                    pe.wait_ge(c_mgs, 1 + ch + 1)
                    for i in range(TI):
                        ins = pe.matmul(turns[:, i * D:(i + 1) * D], mg_t[:, i * P:(i + 1) * P], wo[:, :],
                                        start=True, stop=True)
                    ins.then_inc(c_y, 1)
                if r == 5:
                    pe.wait_ge(c_x1, 1 + ch + 1)
                    for i in range(TI):
                        ins = pe.transpose(turns[:, i * P:(i + 1) * P], x1_w[:, i * P:(i + 1) * P], ident[:, :])
                    ins.then_inc(c_x1t, 1)
                if r == 8:
                    pe.wait_ge(c_hi, 1 + ch + 1)
                    for i in range(TI):
                        ins = pe.matmul(turns[:, i * E:(i + 1) * E], x1_tw[:, i * P:(i + 1) * P], rw[:, :],
                                        start=True, stop=True)
                    ins.then_inc(c_log, 1)

            def experts(ch, n):
                if n < UNITS:
                    if n == 0:
                        pe.wait_ge(c_lo, 1 + ch + 1)
                    pe.wait_ge(f_hid, ch * UNITS + n + 1)
                    for w in range(2):
                        at = slice(w * E * F + n * P, w * E * F + (n + 1) * P)
                        for k, (ws, xs) in enumerate(((w_hi, x1_hi), (w_hi, x1_lo), (w_lo, x1_hi))):
                            ins = pe.matmul(bank[2 * (n % 2) + w][:, :], ws[:, at], xs[:, bass.ds(ch * CH, CH)],
                                            start=k == 0, stop=k == 2)
                    ins.then_inc(f_ab, 1)
                if W2_LAG <= n < UNITS + W2_LAG:
                    m = n - W2_LAG
                    e, f = divmod(m, FT)
                    if f == 0:
                        pe.wait_ge(f_eo, ch * E + e + 1)
                    pe.wait_ge(f_lo, ch * UNITS + m + 1 + HB)
                    at = slice(2 * E * F + m * P, 2 * E * F + (m + 1) * P)
                    for k, (ws, hs) in enumerate(((w_hi, hid_hi), (w_hi, hid_lo), (w_lo, hid_hi))):
                        ins = pe.matmul(bank[4 + e % 2][:, :], ws[:, at], hs[:, m % HB, :],
                                        start=f == 0 and k == 0, stop=f == FT - 1 and k == 2)
                    ins.then_inc(f_w2, 1)
                if n >= TR_STEP and (n - TR_STEP) % FT == 0 and n < TR_STEP + UNITS:
                    e = (n - TR_STEP) // FT
                    pe.wait_ge(f_eo, ch * E + e + 1 + 2)
                    pe.wait_ge(f_y, 1 + ch * E + e)
                    for i in range(TI):
                        ins = pe.transpose(bank[6][:, i * P:(i + 1) * P], eo_sb[:, e % 2, i * P:(i + 1) * P],
                                           ident[:, :])
                    ins.then_inc(f_tr, 1)

            pe.wait_ge(s_reduced, SB + NS * GROUPS)
            pe.wait_ge(w_split, 1 + GROUPS - 2)
            stage(LAST, GROUPS, 0, 0, GROUPS // 2, SMALL_0 + (GROUPS - 1) * SMALL)
            pe.wait_ge(c_top, 2)
            pe.sem_inc(f_w2, HB)
            pe.sem_inc(f_tr, 2)
            for n in range(HEAD):
                experts(0, n)
            pe.wait_ge(small_read, SMALL_0 + GROUPS * SMALL)
            with pe.Fori(0, CHUNKS - 1) as i:
                for n in range(HEAD, HEAD + UNITS):
                    if n >= UNITS:
                        experts(i + 1, n - UNITS)
                    experts(i, n)
                    between(i + 1, n - HEAD)
            for n in range(HEAD, Z_STEP + 1):
                experts(CHUNKS - 1, n)


def kernel(**inputs):
    import concourse.bacc as bacc
    from concourse.bass_utils import run_bass_kernel_spmd

    x = np.ascontiguousarray(inputs["L0_attn_x"])
    tokens = x.reshape(T, D)
    w1 = inputs["L0_ffn_w1"].transpose(1, 0, 2).reshape(D, E * F)
    w3 = inputs["L0_ffn_w3"].transpose(1, 0, 2).reshape(D, E * F)
    w2 = inputs["L0_ffn_w2"].reshape(E * FT, P, D).transpose(1, 0, 2).reshape(P, E * F)
    inv_freq = np.float32(1.0) / np.float32(10000.0) ** (np.arange(0, DH, 2, dtype=np.float32) / np.float32(DH))
    freq = (np.arange(S, dtype=np.float32)[:, None] * inv_freq[None, :]).astype(np.float32)
    row = (np.arange(D) % DH) // 2
    arrays = {
        "x_tok": tokens, "x_feat": np.ascontiguousarray(tokens.T),
        "qw": inputs["L0_attn_qw"], "kw": inputs["L0_attn_kw"], "vw": inputs["L0_attn_vw"], "ow": inputs["L0_attn_ow"],
        "router_w": inputs["L0_ffn_router_w"], "router_b": inputs["L0_ffn_router_b"],
        "w_all": np.concatenate([w1, w3, w2], axis=1),
        "cos_t": np.cos(freq).T[row], "sin_t": np.sin(freq).T[row],
        "ident": np.eye(P, dtype=np.float32),
        "mask": np.where(np.arange(QD)[None, :] > (np.arange(P) % QD)[:, None], np.float32(MASKED), np.float32(0)),
        "tri": np.broadcast_to(np.stack([np.triu(np.ones((E, E), np.float32), 1).ravel(),
                                         np.tril(np.ones((E, E), np.float32), -1).ravel()]), (P, 2, E * E)),
    }
    arrays = {n: np.ascontiguousarray(a) for n, a in arrays.items()}
    nc = bacc.Bacc("TRN2", target_bir_lowering=False, num_devices=1)
    args = [nc.dram_tensor(f"in_{n}", a.shape, mybir.dt.from_np(a.dtype), kind="ExternalInput").ap()
            for n, a in arrays.items()]
    out = nc.dram_tensor("out_tokens", (T, D), F32, kind="ExternalOutput").ap()
    transformer_block(nc, *args, out)
    r = run_bass_kernel_spmd(nc, [{f"in_{n}": a for n, a in arrays.items()}], core_ids=[0])
    return r.results[0]["out_tokens"].reshape(B, S, D)
```

```python
from contextlib import ExitStack

import numpy as np

import concourse.bass as bass
from concourse import mybir

F32 = mybir.dt.float32
F32R = mybir.dt.float32r
BF16 = mybir.dt.bfloat16
ALU = mybir.AluOpType
ACT = mybir.ActivationFunctionType
AX = mybir.AxisListType

P = 128
B, S, D = 2, 1024, 128
H = 16
DH = D // H
E, F = 4, 512
T = B * S
EPS = 1e-5

GH = 4
QD = P // GH
NG = H // GH
GROUPS = B * NG
CH = 512
NC = S // CH
CHUNKS = T // CH
TI = CH // P
NB = CH // QD
KT = S // P
QROWS = 3 * DH + 2
KROWS = 3 * DH
MASKED = -1e30
FT = F // P
UNITS = E * FT

S_UNITS = [(0, j, 0) for j in range(CH // QD)]
S_UNITS += [(1, j, half) for j in range(CH // QD, S // QD) for half in range(2)]
T_UNITS = [(c, kt, h) for c in range(NC) for kt in range(TI * (c + 1)) for h in range(GH)]
NS = len(S_UNITS)
NT = len(T_UNITS)
SEG_S = [sum(u[0] == c for u in S_UNITS) for c in range(NC)]
SEG_T = [sum(u[0] == c for u in T_UNITS) for c in range(NC)]
NPV = NT // GH
SB = 3
TB = 3
HB = 4
PB = 3


C_STEPS = 15
C_FROM, C_EVERY = 4, 3


PROJ_FIRST = 6
PROJ_AT = (6, 14, 20)
V_AT = (10, 17, 19)
S_LATE, S_EARLY = 0, 3
MROWS_AT, NORM_AT, MROWS0_AT, NORM0_AT = 5, 12, 19, 25


def stage_plan(with_s, with_t):
    s_units = S_UNITS if with_s else []
    t_units = [(u, 0) for u in T_UNITS[GH:]] if with_t else []
    t_units += [(u, 1) for u in T_UNITS[:GH]] if with_s else []

    def s_work(units):
        return sum(60 + min(CH, QD * (j + 1) - half * CH) for _, j, half in units)

    def t_work(units):
        return sum(60 + CH - P * max(0, kt - TI * c) for (c, kt, _), _ in units)

    plan = []
    done_s = 0
    if not with_t:
        for unit in s_units:
            if done_s in PROJ_AT:
                plan.append(("P", PROJ_FIRST + PROJ_AT.index(done_s)))
            if done_s in V_AT:
                plan.append(("V", 1 + V_AT.index(done_s)))
            plan.append(("S", *unit))
            done_s += 1
            if done_s == SEG_S[0] + 5:
                plan.append(("MROWS", 0))
    for x, ((c, kt, h), ahead) in enumerate(t_units):
        at = T_UNITS.index((c, kt, h)) + NT * ahead
        plan.append(("T", c, kt, h, ahead))
        if not with_s and at >= C_FROM and (at - C_FROM) % C_EVERY == 0 and (at - C_FROM) // C_EVERY < C_STEPS:
            plan.append(("C", (at - C_FROM) // C_EVERY))
        part = min(1, t_work(t_units[S_LATE:x + 1]) / max(1, t_work(t_units[S_LATE:len(t_units) - S_EARLY])))
        while done_s < len(s_units) and s_work(s_units[:done_s + 1]) <= part * s_work(s_units):
            plan.append(("S", *s_units[done_s]))
            done_s += 1
        if h == GH - 1 and with_t and not with_s:
            t = at // GH - 2
            if t >= 0:
                plan.append(("PV", int(t >= TI), t - TI * (t >= TI)))
            if t == TI - 1:
                plan.append(("OCOPY", 0))
        elif h == GH - 1 and with_t:
            if kt >= 1:
                plan.append(("PV", c, kt - 1))
            else:
                before = NC - 1 if ahead else c - 1
                plan.append(("PV", before, TI * (before + 1) - 1))
                plan.append(("OCOPY", before))
        if with_t and at == MROWS_AT:
            plan.append(("MROWS", NC - 1))
        if with_t and at == NORM_AT:
            plan.append(("NORM", NC - 1))
        if with_s and with_t and at == MROWS0_AT:
            plan.append(("MROWS", 0))
        if with_t and at == NORM0_AT:
            plan.append(("NORM", 0))
    assert done_s == len(s_units)
    if not with_s:
        plan += [("PV", NC - 1, KT - 2), ("PV", NC - 1, KT - 1)]
        plan.append(("OCOPY", NC - 1))
        plan.append(("NORM", NC - 1))
    plan.append(("END",))
    uses = iter(range(len(plan)))
    return [(*step, next(uses)) if step[0] in ("MROWS", "NORM") else step for step in plan]


PROLOGUE = stage_plan(True, False)
STEADY = stage_plan(True, True)
LAST = stage_plan(False, True)
SMALL_0 = sum(x[0] in ("MROWS", "NORM") for x in PROLOGUE)
SMALL = sum(x[0] in ("MROWS", "NORM") for x in STEADY)
PIECE = 3 * E * F // (GROUPS - 2)
assert NS % SB == 0 and NT % TB == 0 and NPV % PB == 0


W2_LAG = 3
EO_STEP = FT - 1 + W2_LAG
TR_STEP = Y_STEP = EO_STEP + 1
STAT_STEP = Y_STEP + UNITS - FT + 1
VAR_STEP = RSTD_STEP = STAT_STEP + 1
Z_STEP = VAR_STEP + 1
HEAD = Z_STEP + 1 - UNITS
assert C_STEPS <= UNITS and Y_STEP + UNITS > Z_STEP


def transformer_block(nc, x_tok, x_feat, qw, kw, vw, ow, router_w, router_b, w_all,
                      cos_t, sin_t, ident_d, mask_d, tri_d, out):
    nc.disable_value_cache = True
    ctx = ExitStack()
    with ctx:
        def sb(name, shape, dt=F32):
            return ctx.enter_context(nc.sbuf_tensor(name, shape, dt))

        def sem(name):
            return ctx.enter_context(nc.semaphore(name))

        bank = [ctx.enter_context(nc.psum_tensor(f"bank{i}", [P, CH], F32)) for i in range(8)]
        s_bank, t_bank, o_bank, small_bank = bank[0:3], bank[3:6], bank[6], bank[7]

        q_dram = nc.dram_tensor("q_scratch", (B * H, QROWS, S), F32).ap()
        k_dram = nc.dram_tensor("k_scratch", (B * H, QD, S), F32).ap()

        cos_sb, sin_sb = sb("cos_sb", [P, S]), sb("sin_sb", [P, S])
        ident = sb("ident", [P, P])
        mask_f = sb("mask_f", [P, QD])
        ident_b, mask_b = sb("ident_b", [P, P], BF16), sb("mask_b", [P, QD], BF16)
        tri = sb("tri", [P, 2, E * E])
        wqk = sb("wqk", [P, 4, D])
        wv, wo = sb("wv", [P, D]), sb("wo", [P, D])
        rw, rb = sb("rw", [P, E]), sb("rb", [P, E])
        xT = sb("xT", [P, T])
        x_res = sb("x_res", [P, T // P, D])
        w_raw = sb("w_raw", [P, PIECE])
        w_hi, w_lo = sb("w_hi", [P, 3 * E * F], F32R), sb("w_lo", [P, 3 * E * F], F32R)

        by_cos, by_sin = sb("by_cos", [P, 2, CH]), sb("by_sin", [P, 2, CH])
        roped = sb("roped", [P, 2, CH])
        rope_hi, rope_lo = sb("rope_hi", [P, 2, CH]), sb("rope_lo", [P, 2, CH])

        q_op = [sb(f"q_op{u}", [P, S // QD, GH, QD], F32R) for u in range(2)]
        k_op = [sb(f"k_op{u}", [P, S], F32R) for u in range(2)]
        v_op = [sb(f"v_op{u}", [P, KT, GH, QD]) for u in range(2)]
        num = sb("num", [P, PB, GH, CH])
        maxima = sb("maxima", [P, 2, S // QD])
        neg_max = [sb(f"neg_max{c}", [P, 2 * CH // QD]) for c in range(NC)]
        max_rows = [sb(f"max_rows{c}", [2 * CH // QD, P]) for c in range(NC)]
        o_sb = [sb(f"o_sb{c}", [P, CH]) for c in range(NC)]
        rden = sb("rden", [P, TI, GH])
        merged = sb("merged", [P, GROUPS + 1, S // P, QD])
        v_tok = sb("v_tok", [P, T // P, D])

        mg_w, mg_t, x1_w, x1_tw = (sb(n, [P, CH]) for n in ("mg_w", "mg_t", "x1_w", "x1_tw"))
        resid = sb("resid", [P, CH])
        x1 = xT[:, :].rearrange("p (t d) -> p t d", d=D)
        flat = [q_op[u][:, :, :, :].rearrange("p j h q -> p (j h q)") for u in range(2)]
        x1_hi, x1_lo = flat[0][:, 0:T], flat[0][:, T:2 * T]
        stats, mv = sb("stats", [P, TI, 6]), sb("mv", [P, TI, 2])
        veps, rstd, minus_half = sb("veps", [P, TI]), sb("rstd", [P, TI]), sb("minus_half", [P, TI])
        logits = sb("logits", [P, TI, E])
        gt, ge = sb("gt", [P, TI, E, E]), sb("ge", [P, TI, E, E])
        rank, chosen = sb("rank", [P, TI, E]), sb("chosen", [P, TI, E])
        top, gate_w, second = sb("top", [P, TI]), sb("gate_w", [P, TI, E]), sb("second", [P, TI])
        gates = sb("gates", [P, T // P, E])
        hid_hi, hid_lo = (flat[1][:, i * HB * CH:(i + 1) * HB * CH].rearrange("p (n t) -> p n t", n=HB)
                          for i in range(2))
        hid, silu_sb, eo_sb = num[:, 0, :, :], num[:, 1, 0:2, :], num[:, 1, 2:4, :]
        y_sb, z_sb = (num[:, 2, i, :].rearrange("p (i d) -> p i d", i=TI) for i in range(2))

        ld_proj, ld_v, ld_res, ld_small = (sem(n) for n in ("ld_proj", "ld_v", "ld_res", "ld_small"))
        ld_tab = [sem(f"ld_tab{c}") for c in range(NC)]
        ld_x = [sem(f"ld_x{ch}") for ch in range(CHUNKS)]
        ld_w = sem("ld_w")
        zeros_stored = sem("zeros_stored")
        ops_filled = sem("ops_filled")
        q_loaded = [[sem(f"q_loaded{u}{c}") for c in range(NC)] for u in range(2)]
        k_loaded = [[sem(f"k_loaded{u}{c}") for c in range(NC)] for u in range(2)]
        v_laid = [sem(f"v_laid{u}") for u in range(2)]
        rot_ready, proj_ready, turned, roped_ready, hi_ready, lo_ready = (sem(n) for n in (
            "rot_ready", "proj_ready", "turned", "roped_ready", "hi_ready", "lo_ready"))
        hilo_stored = [sem(f"hilo_stored{i}") for i in range(2)]
        v_proj, v_cleared, v_copied = (sem(n) for n in ("v_proj", "v_cleared", "v_copied"))
        s_ready, s_reduced = sem("s_ready"), sem("s_reduced")
        t_ready, t_exped = sem("t_ready"), sem("t_exped")
        masked, pv_done, o_copied = sem("masked"), sem("pv_done"), sem("o_copied")
        max_split, small_ready, small_read = sem("max_split"), sem("small_ready"), sem("small_read")
        rows_loaded = [sem(f"rows_loaded{c}") for c in range(NC)]
        dve_step, dve_turn, pool_turn = sem("dve_step"), sem("dve_turn"), sem("pool_turn")
        w_split, w_hi_done, small_cast = sem("w_split"), sem("w_hi_done"), sem("small_cast")
        c_mg, c_mgt, c_mgs, c_y, c_var, c_rstd, c_x1, c_x1t, c_hi, c_log, c_lo, c_tanh, c_store, c_top = (
            sem(n) for n in ("c_mg", "c_mgt", "c_mgs", "c_y", "c_var", "c_rstd", "c_x1", "c_x1t",
                             "c_hi", "c_log", "c_lo", "c_tanh", "c_store", "c_top"))
        c_done, c_x1s = sem("c_done"), sem("c_x1s")
        f_ab, f_silu, f_hid, f_hi, f_lo, f_eo, f_tr, f_y = (sem(n) for n in (
            "f_ab", "f_silu", "f_hid", "f_hi", "f_lo", "f_eo", "f_tr", "f_y"))
        f_w2 = sem("f_w2")
        c_step, f_step = sem("c_step"), sem("f_step")
        f_var, f_rstd, f_z = sem("f_var"), sem("f_rstd"), sem("f_z")
        out_stored = sem("out_stored")

        block = ctx.enter_context(nc.Block())

        @block.sync
        def _(sp):
            sp.sem_inc(out_stored, 16)
            for w, i in ((qw, 0), (kw, 2)):
                sp.dma_start(wqk[:, i, :], w).then_inc(ld_proj, 16)
            for ch in range(CHUNKS):
                sp.dma_start(xT[:, ch * CH:(ch + 1) * CH], x_feat[:, ch * CH:(ch + 1) * CH]).then_inc(ld_x[ch], 16)
                if ch < NC:
                    cols = slice(ch * CH, (ch + 1) * CH)
                    sp.dma_start(cos_sb[:, cols], cos_t[:, cols]).then_inc(ld_tab[ch], 16)
                    sp.dma_start(sin_sb[:, cols], sin_t[:, cols]).then_inc(ld_tab[ch], 16)
                if ch == 0:
                    sp.dma_start(wv[:, :], vw).then_inc(ld_v, 16)
            for dst, src in ((ident[:, :], ident_d), (mask_f[:, :], mask_d)):
                sp.dma_start(dst, src).then_inc(ld_small, 16)
            sp.wait_ge(ops_filled, 1)
            sp.dma_start(q_dram[:, KROWS:QROWS, :],
                         flat[0][0:B * H * 2, 0:S].bitcast(F32))\
                .then_inc(zeros_stored, 16)
            sp.wait_ge(ops_filled, 2)
            for b in range(B):
                sp.dma_start(k_dram[b * H:(b + 1) * H, KROWS:QD, :], k_op[0][:, :].bitcast(F32))\
                    .then_inc(zeros_stored, 16)

            def load_q(n, u, c):
                for h in range(GH):
                    sp.dma_start(q_op[u][h * QD:h * QD + QROWS, c * NB:(c + 1) * NB, h, :].bitcast(F32),
                                 q_dram[bass.ds(n * GH + h, 1), :, c * CH:(c + 1) * CH]
                                 .rearrange("g r t -> (g r) t")).then_inc(q_loaded[u][c], 16)

            def load_k(n, u, c):
                sp.dma_start(k_op[u][:, c * CH:(c + 1) * CH].bitcast(F32),
                             k_dram[bass.ds(n * GH, GH), :, c * CH:(c + 1) * CH]
                             .rearrange("g r t -> (g r) t")).then_inc(k_loaded[u][c], 16)

            def store(n):
                ch, is_k = divmod(n, 2)
                b, c = divmod(ch, NC)
                cols = slice(c * CH, (c + 1) * CH)
                heads = slice(b * H, (b + 1) * H)
                dram = k_dram if is_k else q_dram
                hi_at, lo_at = ((0, 2), 1) if is_k else ((0, 1), 2)
                sp.wait_ge(hi_ready, n + 1)
                for r in hi_at:
                    sp.dma_start(dram[heads, r * DH:(r + 1) * DH, cols],
                                 rope_hi[:, n % 2, :])\
                        .then_inc(hilo_stored[n % 2], 16)
                sp.wait_ge(lo_ready, n + 1)
                sp.dma_start(dram[heads, lo_at * DH:(lo_at + 1) * DH, cols],
                             rope_lo[:, n % 2, :])\
                    .then_inc(hilo_stored[n % 2], 16)

            def stored(chunks):
                for i in range(2):
                    sp.wait_ge(hilo_stored[i], 3 * 16 * chunks)

            for n in range(2 * NC):
                store(n)
                if n == 2 * NC - 2:
                    sp.wait_ge(zeros_stored, 16 * (1 + B))
                    stored(1)
                    load_q(0, 0, 0)
                    load_k(0, 0, 0)
            stored(NC)
            load_q(0, 0, 1)
            load_k(0, 0, 1)
            for n in range(2 * NC, 2 * CHUNKS):
                store(n)
            sp.wait_ge(ops_filled, 3)
            for c in range(NC):
                load_q(1, 1, c)
                load_k(1, 1, c)
            stored(CHUNKS)
            for dst, src in ((wo[:, :], ow), (rw[:, :], router_w),
                             (tri[:, :, :], tri_d), (rb[:, :], router_b.partition_broadcast(P))):
                sp.dma_start(dst, src).then_inc(ld_small, 16)
            sp.dma_start(x_res[:, :, :], x_tok.rearrange("(t p) d -> p t d", p=P)).then_inc(ld_res, 16)

            def stage(plan, s, u, small, load=False):
                n = s - 1
                v = 1 - u
                for step in plan:
                    if step[0] == "MROWS":
                        _, c, use = step
                        to = u if (c == 0 or plan is PROLOGUE) else v
                        sp.wait_ge(small_read, small + use + 1)
                        for h in range(GH):
                            sp.dma_start(
                                q_op[to][h * QD + KROWS:h * QD + QROWS, c * NB:(c + 1) * NB, h, :].bitcast(F32),
                                max_rows[c][:, h * QD:(h + 1) * QD])\
                                .then_inc(rows_loaded[c], 16)
                    if not load:
                        continue
                    if step == ("T", 1, 0, 0, 0):
                        sp.wait_ge(t_ready, NT * n + SEG_T[0])
                        load_q(s + 1, v, 0)
                    if step == ("T", 1, TI, 0, 0):
                        sp.wait_ge(t_ready, NT * n + SEG_T[0] + TI * GH)
                        load_k(s + 1, v, 0)
                        sp.wait_ge(w_split, 1 + n)
                        sp.dma_start(w_raw[:, :], w_all[:, bass.ds(n * PIECE, PIECE)]).then_inc(ld_w, 16)
                    if step == ("END",):
                        sp.wait_ge(t_ready, NT * n + NT)
                        load_q(s + 1, v, 1)
                        load_k(s + 1, v, 1)

            stage(PROLOGUE, 0, 0, 0)
            with sp.Fori(0, GROUPS // 2 - 1) as i:
                stage(STEADY, i * 2 + 1, 1, i * (2 * SMALL) + SMALL_0, load=True)
                stage(STEADY, i * 2 + 2, 0, i * (2 * SMALL) + SMALL_0 + SMALL, load=True)
            stage(STEADY, GROUPS - 1, 1, SMALL_0 + (GROUPS - 2) * SMALL)
            stage(LAST, GROUPS, 0, SMALL_0 + (GROUPS - 1) * SMALL)

            with sp.Fori(0, CHUNKS) as ch:
                sp.wait_ge(f_z, 1 + ch + 1)
                sp.dma_start(out[bass.ds(ch * CH, CH), :].rearrange("(t p) d -> p t d", p=P), z_sb[:, :, :])\
                    .then_inc(out_stored, 16)
            sp.wait_ge(out_stored, 16 * CHUNKS + 16)

        @block.gpsimd
        def _(pool):
            for credit in (w_split,):
                pool.sem_inc(credit, 1)
            pool.memset(flat[0].bitcast(F32), 0.0).then_inc(ops_filled, 1)
            pool.memset(k_op[0][:, :].bitcast(F32), 1.0).then_inc(ops_filled, 1)
            for n in range(2 * CHUNKS):
                pool.wait_ge(turned, n + 1)
                if n >= 2:
                    pool.wait_ge(lo_ready, n - 1)
                pool.tensor_tensor(roped[:, n % 2, :], by_cos[:, n % 2, :], by_sin[:, n % 2, :], ALU.add)\
                    .then_inc(roped_ready, 1)
            pool.memset(flat[1].bitcast(F32), 0.0).then_inc(ops_filled, 1)
            pool.memset(o_sb[NC - 1][:, :], 1.0).then_inc(ops_filled, 1)
            pool.memset(minus_half[:, :], -0.5).then_inc(ops_filled, 1)

            def lay_v(g, b, u):
                pool.tensor_copy(v_op[u][:, :, :, 0:DH],
                                 v_tok[:, bass.ds(b * KT, KT), bass.ds(g * GH * DH, GH * DH)]
                                 .rearrange("p k (h d) -> p k h d", h=GH)).then_inc(v_laid[u], 1)

            def stage(plan, n, u, split=False):
                for step in plan:
                    if plan is STEADY and step == ("T", 1, 1, 0, 0):
                        pool.wait_ge(pv_done, PB + NPV * n)
                        lay_v((n + 1) % NG, (n + 1) // NG, u)
                    if step[0] == "C":
                        between(0, step[1], first=True)
                    if step[0] != "T":
                        continue
                    _, c, kt, h, ahead = step
                    if kt >= TI * c and h == GH - 1:
                        k = NT * ahead + T_UNITS.index((c, kt, h))
                        off = P * (kt - TI * c)
                        pool.wait_ge(t_exped, TB + NT * n + k + 1)
                        pool.sem_inc(pool_turn, 1)
                        tile = num[:, (k // GH) % PB, :, off:off + P]
                        pool.affine_select(out=tile, in_=tile, compare_op=ALU.is_ge, fill=0.0, base=0,
                                           pattern=[[0, GH], [1, P]], channel_multiplier=-1)\
                            .then_inc(masked, 1)
                    if split and step == ("T", 0, 0, GH - 1, 1):
                        pool.wait_ge(w_hi_done, n + 1)
                        pool.tensor_tensor(w_lo[:, bass.ds(n * PIECE, PIECE)], w_raw[:, :],
                                           w_hi[:, bass.ds(n * PIECE, PIECE)].bitcast(F32), ALU.subtract)\
                            .then_inc(w_split, 1)

            pool.wait_ge(v_cleared, 4)
            pool.wait_ge(v_copied, CHUNKS)
            lay_v(0, 0, 0)
            stage(PROLOGUE, -1, 0)
            with pool.Fori(0, GROUPS // 2 - 1) as i:
                stage(STEADY, i * 2, 1, split=True)
                stage(STEADY, i * 2 + 1, 0, split=True)
            stage(STEADY, GROUPS - 2, 1)

            def between(ch, r, first=False):
                if r == 3:
                    pool.wait_ge(c_var, ch + 1)
                    pool.tensor_tensor(rstd[:, :], veps[:, :], minus_half[:, :], ALU.pow).then_inc(c_rstd, 1)

            def experts(ch, n):
                if 1 <= n <= UNITS:
                    m = n - 1
                    pool.wait_ge(f_hi, ch * UNITS + m + 1)
                    pool.wait_ge(f_w2, ch * UNITS + m + 1)
                    pool.tensor_tensor(hid_lo[:, m % HB, :], hid[:, m % HB, :], hid_hi[:, m % HB, :].bitcast(F32),
                                       ALU.subtract).then_inc(f_lo, 1)
                if n == RSTD_STEP:
                    pool.wait_ge(f_var, ch + 1)
                    pool.tensor_tensor(rstd[:, :], veps[:, :], minus_half[:, :], ALU.pow).then_inc(f_rstd, 1)

            pool.wait_ge(ops_filled, 5)
            stage(LAST, GROUPS - 1, 0)
            for n in range(HEAD):
                experts(0, n)
            with pool.Fori(0, CHUNKS - 1) as i:
                for n in range(HEAD, HEAD + UNITS):
                    if n >= UNITS:
                        experts(i + 1, n - UNITS)
                    experts(i, n)
                    between(i + 1, n - HEAD)
            for n in range(HEAD, Z_STEP + 1):
                experts(CHUNKS - 1, n)

        @block.scalar
        def _(act):
            for credit in (c_hi, c_mgs, c_store, o_copied):
                act.sem_inc(credit, 1)
            act.wait_ge(ld_proj, 32)
            for i in (0, 2):
                pair = wqk[:, i, :].rearrange("p (n two) -> p n two", two=2)
                turn = wqk[:, i + 1, :].rearrange("p (n two) -> p n two", two=2)
                act.activation(turn[:, :, 0], pair[:, :, 1], ACT.Copy, scale=-1.0)
                act.activation(turn[:, :, 1], pair[:, :, 0], ACT.Copy).then_inc(rot_ready, 1)

            def copy_v(ch):
                act.wait_ge(v_proj, ch + 1)
                act.activation(v_tok[:, ch * TI:(ch + 1) * TI, :].rearrange("p k d -> p (k d)"),
                               bank[3][:, :], ACT.Copy).then_inc(v_copied, 1)

            for n in range(2 * CHUNKS):
                if n == 4:
                    act.wait_ge(ld_small, 16 * 2)
                    act.activation(ident_b[:, :], ident[:, :], ACT.Copy).then_inc(small_cast, 1)
                    act.activation(mask_b[:, :], mask_f[:, :], ACT.Copy).then_inc(small_cast, 1)
                if n in (PROJ_FIRST - 1, PROJ_FIRST + 1):
                    copy_v((n - PROJ_FIRST + 1) // 2)
                act.wait_ge(roped_ready, n + 1)
                if n >= 2:
                    act.wait_ge(hilo_stored[n % 2], 3 * 16 * (n // 2))
                act.activation(rope_hi[:, n % 2, :].bitcast(F32R), roped[:, n % 2, :], ACT.Copy)\
                    .then_inc(hi_ready, 1)
            copy_v(2)
            copy_v(3)
            act.sem_inc(t_exped, TB)

            def stage(plan, n, split=False):
                scale = float(DH) ** -0.5
                for step in plan:
                    if split and step == ("T", 0, 0, 0, 1):
                        act.wait_ge(ld_w, (n + 1) * 16)
                        act.activation(w_hi[:, bass.ds(n * PIECE, PIECE)], w_raw[:, :], ACT.Copy)\
                            .then_inc(w_hi_done, 1)
                    if step[0] == "T":
                        _, c, kt, h, ahead = step
                        k = NT * ahead + T_UNITS.index((c, kt, h))
                        off = P * max(0, kt - TI * c)
                        t = k // GH
                        act.wait_ge(t_ready, NT * n + k + 1)
                        if h == 0:
                            act.wait_ge(pv_done, NPV * n + t + 1)
                        act.activation(num[:, t % PB, h, off:CH], t_bank[k % TB][:, off:CH], ACT.Exp, scale=scale)\
                            .then_inc(t_exped, 1)
                    if step[0] == "OCOPY":
                        c = step[1]
                        act.wait_ge(pv_done, PB + NPV * n + (TI if c == 0 else NPV))
                        act.wait_ge(small_ready, SMALL_0 + SMALL * n + (2 if c == NC - 1 else 0))
                        act.activation(o_sb[c][:, :], o_bank[:, :], ACT.Copy).then_inc(o_copied, 1)
                    if step[0] == "C":
                        between(0, 0, 0, step[1], first=True)

            stage(PROLOGUE, -1)
            with act.Fori(0, GROUPS // 2 - 1) as i:
                stage(STEADY, i * 2, split=True)
                stage(STEADY, i * 2 + 1, split=True)
            stage(STEADY, GROUPS - 2)

            def between(ch, b, c, r, first=False):
                turns = bank[0] if first else bank[7]
                if r == 0:
                    act.wait_ge(small_read, SMALL_0 + (GROUPS - first) * SMALL)
                    act.wait_ge(c_mgt, 1 + ch)
                    act.activation(mg_w[:, :].rearrange("p (i g r) -> p i g r", i=TI, g=NG),
                                   merged[:, bass.ds(b * NG + 1, NG), bass.ds(c * TI, TI), :]
                                   .rearrange("p g i r -> p i g r"), ACT.Copy).then_inc(c_mg, 1)
                if r == 1:
                    act.wait_ge(c_mgt, 1 + ch + 1)
                    act.wait_ge(c_y, 1 + ch)
                    act.activation(mg_t[:, :], turns[:, :], ACT.Copy).then_inc(c_mgs, 1)
                if r == 7:
                    act.wait_ge(c_x1t, 1 + ch + 1)
                    act.activation(x1_hi[:, bass.ds(ch * CH, CH)], turns[:, :], ACT.Copy).then_inc(c_hi, 1)
                if r == 8:
                    act.wait_ge(c_log, 1 + ch)
                    act.wait_ge(c_lo, 1 + ch + 1)
                    act.activation(x1_tw[:, :], turns[:, :], ACT.Copy).then_inc(c_x1s, 1)
                if r == 9:
                    act.wait_ge(c_x1, 1 + ch + 1)
                    act.activation(x1[:, bass.ds(ch * TI, TI), :].rearrange("p i d -> p (i d)"), x1_w[:, :], ACT.Copy)\
                        .then_inc(c_store, 1)
                if r == 12:
                    act.wait_ge(c_top, 1 + ch + 1)
                    act.wait_ge(c_done, ch * 2 + 1)
                    act.activation(gate_w[:, :, :], logits[:, :, :], ACT.Tanh).then_inc(c_tanh, 1)

            def experts_hi(ch, n):
                if 1 <= n <= UNITS:
                    m = n - 1
                    act.wait_ge(f_hid, ch * UNITS + m + 1 + 2)
                    act.wait_ge(f_w2, ch * UNITS + m + 1)
                    act.activation(hid_hi[:, m % HB, :], hid[:, m % HB, :], ACT.Copy).then_inc(f_hi, 1)

            def experts_silu(ch, n):
                if n < UNITS:
                    act.wait_ge(f_ab, ch * UNITS + n + 1)
                    act.wait_ge(f_hid, ch * UNITS + n + 1)
                    act.activation(silu_sb[:, n % 2, :], bank[2 * (n % 2)][:, :], ACT.Silu).then_inc(f_silu, 1)
                if n >= EO_STEP and (n - EO_STEP) % FT == 0 and n < EO_STEP + UNITS:
                    e = (n - EO_STEP) // FT
                    act.wait_ge(f_w2, ch * UNITS + (FT * (e + 1) + HB))
                    act.wait_ge(f_tr, ch * E + e + 1)
                    act.activation(eo_sb[:, e % 2, :], bank[4 + e % 2][:, :], ACT.Copy).then_inc(f_eo, 1)

            stage(LAST, GROUPS - 1)
            act.sem_inc(f_eo, 2)
            for n in range(HEAD):
                experts_hi(0, n)
                experts_silu(0, n)
            with act.Fori(0, CHUNKS - 1) as i:
                for n in range(HEAD, HEAD + UNITS):
                    experts_hi(i, n)
                    if n >= UNITS:
                        experts_hi(i + 1, n - UNITS)
                    between(i + 1, (i + 1) // NC, (i + 1) % NC, n - HEAD)
                    experts_silu(i, n)
                    if n >= UNITS:
                        experts_silu(i + 1, n - UNITS)
            for n in range(HEAD, Z_STEP + 1):
                experts_hi(CHUNKS - 1, n)
                experts_silu(CHUNKS - 1, n)

        @block.vector
        def _(dve):
            for credit in (c_lo, c_done, c_x1, c_top, f_y, f_z):
                dve.sem_inc(credit, 1)
            steps = [0]

            def step_done(ins, looped=None):
                steps[0] += 1
                ins.then_inc(dve_step, 1)
                dve.wait_ge(dve_step, steps[0])

            dve.sem_inc(s_reduced, SB)
            dve.sem_inc(f_hid, 2)
            dve.sem_inc(f_lo, HB)

            for u in range(2):
                dve.memset(v_op[u][:, :, :, :], 0.0).then_inc(v_cleared, 1)
            dve.wait_ge(v_cleared, 2)
            for u in range(2):
                dve.memset(v_op[u][:, :, :, DH:DH + 1], 1.0).then_inc(v_cleared, 1)

            def split_rope(n):
                dve.wait_ge(hi_ready, n + 1)
                if n >= 2:
                    dve.wait_ge(hilo_stored[n % 2], 3 * 16 * (n // 2))
                dve.tensor_tensor(rope_lo[:, n % 2, :].bitcast(F32R), roped[:, n % 2, :], rope_hi[:, n % 2, :],
                                  ALU.subtract).then_inc(lo_ready, 1)

            def rotate(n):
                if n < 2 * CHUNKS:
                    c = n // 2 % NC
                    cols = slice(c * CH, (c + 1) * CH)
                    pair = 4 + 2 * (n % 2)
                    if n in (0, 2):
                        dve.wait_ge(ld_tab[n // 2], 32)
                    dve.wait_ge(proj_ready, n + 1)
                    if n >= 2:
                        dve.wait_ge(roped_ready, n - 1)
                    dve.tensor_tensor(by_cos[:, n % 2, :], bank[pair][:, :], cos_sb[:, cols], ALU.mult)
                    dve.tensor_tensor(by_sin[:, n % 2, :], bank[pair + 1][:, :], sin_sb[:, cols], ALU.mult)\
                        .then_inc(turned, 1)
                if n >= 1:
                    split_rope(n - 1)

            for n in range(PROJ_FIRST):
                rotate(n)

            def split_max(s, c, chain):
                m = CH // QD
                js = slice(c * m, (c + 1) * m)
                top_m = maxima[:, 0, js]
                dve.wait_ge(s_reduced, SB + NS * s + sum(SEG_S[:c + 1]))
                if c > 0:
                    dve.tensor_tensor(top_m, maxima[:, 0, js], maxima[:, 1, js], ALU.max).then_inc(dve_step, 1)
                    dve.wait_ge(dve_step, chain + 1)
                    chain = chain + 1
                dve.tensor_scalar(neg_max[c][:, 0:m].bitcast(F32R), top_m, -1.0, None, ALU.mult).then_inc(dve_step, 1)
                dve.wait_ge(dve_step, chain + 1)
                dve.scalar_tensor_tensor(neg_max[c][:, m:2 * m].bitcast(F32R), top_m, -1.0, neg_max[c][:, 0:m],
                                         ALU.mult, ALU.subtract).then_inc(max_split, 1)

            def stage(plan, s, chain, small):
                done = 0
                for step in plan:
                    if step[0] == "S":
                        _, c, j, half = step
                        k = S_UNITS.index((c, j, half))
                        lo = half * CH
                        width = min(CH, QD * (j + 1) - lo)
                        dve.wait_ge(s_ready, NS * s + k + 1)
                        dve.tensor_reduce(maxima[:, half, j:j + 1], s_bank[k % SB][:, 0:width], AX.X, ALU.max)\
                            .then_inc(s_reduced, 1)
                        done += 1
                        if done == SEG_S[0]:
                            split_max(s, 0, chain)
                            chain = chain + 1
                        if done == NS:
                            split_max(s, 1, chain)
                            chain = chain + 2
                    if step[0] == "P":
                        rotate(step[1])
                    if step[0] == "MROWS":
                        _, c, use = step
                        dve.wait_ge(small_ready, small + use + 1)
                        dve.tensor_copy(max_rows[c][:, :], small_bank[0:2 * CH // QD, 0:P]).then_inc(small_read, 1)
                    if step[0] == "NORM":
                        _, c, use = step
                        slot = s - 1 if c == NC - 1 and use < SMALL - 1 else s
                        view = small_bank[:, :].rearrange("p (i h r) -> p i h r", i=TI, h=GH)
                        dve.wait_ge(small_ready, small + use + 1)
                        dve.reciprocal(rden[:, :, :], view[:, :, :, DH]).then_inc(dve_step, 1)
                        dve.wait_ge(dve_step, chain + 1)
                        chain = chain + 1
                        dve.tensor_tensor(
                            merged[:, bass.ds(slot, 1), c * TI:(c + 1) * TI, :]
                            .rearrange("p g i (h d) -> p (g i) h d", h=GH),
                            view[:, :, :, 0:DH], rden[:, :, :].unsqueeze(3).broadcast_to([P, TI, GH, DH]),
                            ALU.mult).then_inc(small_read, 1)
                    if step[0] == "C":
                        between(0, step[1], first=True)

            CHAIN_0, CHAIN = 3, 3 + NC
            base = steps[0]
            stage(PROLOGUE, 0, base, 0)
            with dve.Fori(0, GROUPS // 2 - 1) as i:
                for u in range(2):
                    stage(STEADY, i * 2 + (1 + u), i * (2 * CHAIN) + (base + CHAIN_0 + u * CHAIN),
                          i * (2 * SMALL) + (SMALL_0 + u * SMALL))
            stage(STEADY, GROUPS - 1, base + CHAIN_0 + (GROUPS - 2) * CHAIN, SMALL_0 + (GROUPS - 2) * SMALL)
            last_base = base + CHAIN_0 + (GROUPS - 1) * CHAIN

            def statistics(src, step_sem):
                for i in range(TI):
                    dve.bn_stats(stats[:, i, :], src(i)).then_inc(step_sem, 1)

            def variance(step_sem, chain, var_sem):
                for i in range(TI):
                    dve.wait_ge(step_sem, chain + (i + 1))
                    dve.sem_inc(dve_turn, 1)
                    dve.bn_aggr(mv[:, i, :], stats[:, i, :]).then_inc(step_sem, 1)
                dve.wait_ge(step_sem, chain + 2 * TI)
                dve.tensor_scalar(veps[:, :], mv[:, :, 1], EPS, None, ALU.add).then_inc(var_sem, 1)

            def normalise(src, dst, done_sem):
                for i in range(TI):
                    ins = dve.tensor_scalar(dst(i), src(i), mv[:, i, 0:1], rstd[:, i:i + 1], ALU.subtract, ALU.mult)
                ins.then_inc(done_sem, 1)

            def between(ch, r, first=False):
                C_CHAIN = 1 + 2 * TI + 12
                turns = bank[0] if first else bank[7]

                def then(ins, k):
                    ins.then_inc(c_step, 1)
                    dve.wait_ge(c_step, ch * C_CHAIN + k)

                k = 1 + 2 * TI
                if r == 1:
                    dve.wait_ge(c_y, 1 + ch + 1)
                    then(dve.tensor_tensor(resid[:, :], turns[:, :],
                                           x_res[:, bass.ds(ch * TI, TI), :].rearrange("p i d -> p (i d)"), ALU.add), 1)
                if r == 2:
                    statistics(lambda i: resid[:, i * D:(i + 1) * D], c_step)
                if r == 3:
                    variance(c_step, ch * C_CHAIN + 1, c_var)
                if r == 5:
                    dve.wait_ge(c_x1t, 1 + ch)
                    dve.wait_ge(c_store, 1 + ch)
                    dve.wait_ge(c_rstd, ch + 1)
                    normalise(lambda i: resid[:, i * D:(i + 1) * D], lambda i: x1_w[:, i * D:(i + 1) * D], c_x1)
                if r == 7:
                    dve.wait_ge(c_hi, 1 + ch + 1)
                    dve.tensor_tensor(x1_lo[:, bass.ds(ch * CH, CH)], turns[:, :],
                                      x1_hi[:, bass.ds(ch * CH, CH)].bitcast(F32), ALU.subtract).then_inc(c_lo, 1)
                a = logits[:, :, :].unsqueeze(2).broadcast_to([P, TI, E, E])
                z = logits[:, :, :].unsqueeze(3).broadcast_to([P, TI, E, E])
                upper = tri[:, 0:1, :].broadcast_to([P, TI, E * E])
                lower = tri[:, 1:2, :].broadcast_to([P, TI, E * E])
                gt_f, ge_f = (m[:, :, :, :].rearrange("p i e j -> p i (e j)") for m in (gt, ge))
                if r == 9:
                    dve.wait_ge(c_log, 1 + ch + 1)
                    then(dve.tensor_tensor(logits[:, :, :], turns[:, 0:TI * E].rearrange("p (i e) -> p i e", i=TI),
                                           rb[:, :].unsqueeze(1).broadcast_to([P, TI, E]), ALU.add), k + 1)
                    then(dve.tensor_tensor(gt[:, :, :, :], a, z, ALU.is_gt), k + 2)
                    then(dve.tensor_tensor(ge[:, :, :, :], a, z, ALU.is_ge), k + 3)
                    then(dve.tensor_tensor(gt_f, gt_f, upper, ALU.mult), k + 4)
                if r == 10:
                    then(dve.tensor_tensor(ge_f, ge_f, lower, ALU.mult), k + 5)
                    then(dve.tensor_tensor(gt_f, gt_f, ge_f, ALU.add), k + 6)
                    then(dve.tensor_reduce(rank[:, :, :], gt[:, :, :, :], AX.X, ALU.add), k + 7)
                    then(dve.tensor_reduce(top[:, :], logits[:, :, :], AX.X, ALU.max), k + 8)
                if r == 11:
                    then(dve.tensor_scalar(chosen[:, :, :], rank[:, :, :], 1.5, None, ALU.is_lt), k + 9)
                    then(dve.tensor_tensor(logits[:, :, :], logits[:, :, :],
                                           top[:, :].unsqueeze(2).broadcast_to([P, TI, E]), ALU.subtract), k + 10)
                    then(dve.tensor_tensor(gate_w[:, :, :], logits[:, :, :], chosen[:, :, :], ALU.mult), k + 11)
                    then(dve.tensor_reduce(second[:, :], gate_w[:, :, :], AX.X, ALU.add), k + 12)
                    dve.scalar_tensor_tensor(logits[:, :, :], second[:, :].unsqueeze(2).broadcast_to([P, TI, E]), -0.5,
                                             logits[:, :, :], ALU.mult, ALU.add).then_inc(c_top, 1)
                if r == C_STEPS - 1:
                    dve.wait_ge(c_tanh, ch + 1)
                    dve.tensor_scalar(gate_w[:, :, :], gate_w[:, :, :], 0.5, 0.5, ALU.mult, ALU.add)\
                        .then_inc(c_done, 1)
                    dve.wait_ge(c_done, 1 + 2 * ch + 1)
                    dve.tensor_tensor(gates[:, bass.ds(ch * TI, TI), :], gate_w[:, :, :], chosen[:, :, :],
                                      ALU.mult).then_inc(c_done, 1)
                    dve.wait_ge(c_done, 1 + 2 * ch + 2)

            def experts(ch, n):
                if n < UNITS:
                    dve.wait_ge(f_silu, ch * UNITS + n + 1)
                    dve.wait_ge(f_lo, ch * UNITS + n + 1)
                    dve.tensor_tensor(hid[:, n % HB, :], bank[2 * (n % 2) + 1][:, :], silu_sb[:, n % 2, :],
                                      ALU.mult).then_inc(f_hid, 1)
                if n >= Y_STEP and (n - Y_STEP) % FT == 0 and n < Y_STEP + UNITS:
                    e = (n - Y_STEP) // FT
                    dve.wait_ge(f_tr, ch * E + e + 1 + 2)
                    dve.wait_ge(f_y, 1 + ch * E + e)
                    if e == 0:
                        dve.wait_ge(f_z, ch + 1)
                        dve.wait_ge(c_store, 1 + ch + 1)
                    for i in range(TI):
                        before = y_sb[:, i, :] if e else \
                            x1[:, bass.ds(ch * TI + i, 1), :].rearrange("p i d -> p (i d)")
                        ins = dve.scalar_tensor_tensor(
                            y_sb[:, i, :], bank[6][:, i * D:(i + 1) * D],
                            gates[:, bass.ds(ch * TI + i, 1), e:e + 1].rearrange("p i e -> p (i e)"),
                            before, ALU.mult, ALU.add)
                    ins.then_inc(f_y, 1)
                if n == STAT_STEP:
                    dve.wait_ge(f_y, 1 + ch * E + E)
                    statistics(lambda i: y_sb[:, i, :], f_step)
                if n == VAR_STEP:
                    variance(f_step, ch * (2 * TI), f_var)
                if n == Z_STEP:
                    dve.wait_ge(out_stored, ch * 16 + 16)
                    dve.wait_ge(f_rstd, ch + 1)
                    normalise(lambda i: y_sb[:, i, :], lambda i: z_sb[:, i, :], f_z)

            dve.wait_ge(ld_small, 16 * 6)
            dve.wait_ge(ld_res, 16)
            stage(LAST, GROUPS, last_base, SMALL_0 + (GROUPS - 1) * SMALL)
            for n in range(HEAD):
                experts(0, n)
            with dve.Fori(0, CHUNKS - 1) as i:
                for n in range(HEAD, HEAD + UNITS):
                    if n >= UNITS:
                        experts(i + 1, n - UNITS)
                    experts(i, n)
                    between(i + 1, n - HEAD)
            for n in range(HEAD, Z_STEP + 1):
                experts(CHUNKS - 1, n)

        @block.tensor
        def _(pe):
            for credit in (c_mgt, c_y, c_log, c_x1t):
                pe.sem_inc(credit, 1)
            pe.wait_ge(rot_ready, 2)

            def project(n):
                ch, is_k = divmod(n, 2)
                if n >= 2:
                    pe.wait_ge(turned, n - 1)
                if not is_k:
                    pe.wait_ge(ld_x[ch], 16)
                for turn in range(2):
                    ins = pe.matmul(bank[4 + 2 * (n % 2) + turn][:, :], wqk[:, 2 * is_k + turn, :],
                                    xT[:, ch * CH:(ch + 1) * CH], start=True, stop=True)
                ins.then_inc(proj_ready, 1)

            def project_v(ch):
                if ch == 0:
                    pe.wait_ge(ld_v, 16)
                else:
                    pe.wait_ge(v_copied, ch)
                for i in range(TI):
                    ins = pe.matmul(bank[3][:, i * D:(i + 1) * D],
                                    xT[:, ch * CH + i * P:ch * CH + (i + 1) * P], wv[:, :], start=True, stop=True)
                ins.then_inc(v_proj, 1)

            for n in range(PROJ_FIRST + 1):
                project(n)
                if n == PROJ_FIRST - 2:
                    project_v(0)
            pe.wait_ge(ld_small, 16 * 2)
            pe.wait_ge(small_cast, 2)
            pe.sem_inc(pv_done, PB)

            def stage(plan, s, u, turn_u, turn_v, small):
                n = s - 1
                v = 1 - u
                seen = set()

                def once(semaphore, value, key):
                    if key not in seen:
                        seen.add(key)
                        pe.wait_ge(semaphore, value)

                for step in plan:
                    if step[0] == "S":
                        _, c, j, half = step
                        k = S_UNITS.index((c, j, half))
                        once(q_loaded[u][c], turn_u * (16 * GH), ("q", c))
                        once(k_loaded[u][half], turn_u * 16, ("k", half))
                        lo = half * CH
                        width = min(CH, QD * (j + 1) - lo)
                        diagonal = QD * (j + 1) - lo <= CH
                        pe.wait_ge(s_reduced, NS * s + k + 1)
                        ins = pe.matmul(s_bank[k % SB][:, 0:width], q_op[u][:, j, :, :].rearrange("p h q -> p (h q)"),
                                        k_op[u][:, lo:lo + width], start=True, stop=not diagonal)
                        if diagonal:
                            ins = pe.matmul(s_bank[k % SB][:, width - QD:width], ident_b[:, :], mask_b[:, :],
                                            start=False, stop=True)
                        ins.then_inc(s_ready, 1)
                    if step[0] == "P":
                        if step[1] + 1 < 2 * CHUNKS:
                            project(step[1] + 1)
                        else:
                            pe.wait_ge(turned, step[1])
                    if step[0] == "V":
                        project_v(step[1])
                    if plan is PROLOGUE and step == ("T", 0, 0, 0, 1):
                        pe.wait_ge(v_copied, CHUNKS)
                    if step[0] == "T":
                        _, c, kt, h, ahead = step
                        w = u if ahead else v
                        k = NT * ahead + T_UNITS.index((c, kt, h))
                        off = P * max(0, kt - TI * c)
                        once(rows_loaded[c], (n + ahead + 1) * (16 * GH), ("m", c, ahead))
                        pe.wait_ge(t_exped, NT * n + k + 1)
                        pe.matmul(t_bank[k % TB][:, off:CH].rearrange("p (j q) -> p j q", q=QD),
                                  k_op[w][:, kt * P:(kt + 1) * P],
                                  q_op[w][:, c * NB + off // QD:(c + 1) * NB, h, :], start=True, stop=True)\
                            .then_inc(t_ready, 1)
                    if step[0] == "PV":
                        _, c, kt = step
                        t = kt + (TI if c > 0 else 0)
                        off = P * max(0, kt - TI * c)
                        once(v_laid[v], turn_v, "v")
                        if kt == 0:
                            pe.wait_ge(o_copied, 1 + NC * n + c)
                        pe.wait_ge(t_exped, TB + NT * n + GH * (t + 1))
                        if kt >= TI * c:
                            pe.wait_ge(masked, NC * TI * n + kt + 1)
                        for h in range(GH):
                            ins = pe.matmul(o_bank[h * QD:(h + 1) * QD, off:CH], v_op[v][:, kt, h, :],
                                            num[:, t % PB, h, off:CH], start=kt == 0, stop=kt == TI * (c + 1) - 1,
                                            tile_position=(0, h * QD))
                        ins.then_inc(pv_done, 1)
                    if step[0] == "MROWS":
                        _, c, use = step
                        g = s if (c == 0 or plan is PROLOGUE) else n
                        pe.wait_ge(max_split, NC * g + c + 1)
                        pe.wait_ge(small_read, small + use)
                        pe.transpose(small_bank[0:2 * CH // QD, 0:P], neg_max[c][:, :], ident[:, :])\
                            .then_inc(small_ready, 1)
                    if step[0] == "NORM":
                        _, c, use = step
                        mine = c == 0 or use == SMALL - 1
                        pe.wait_ge(o_copied, 1 + NC * n + ((c + 1) if mine else 0))
                        pe.wait_ge(small_read, small + use)
                        for i in range(TI):
                            ins = pe.transpose(small_bank[:, i * P:(i + 1) * P], o_sb[c][:, i * P:(i + 1) * P],
                                               ident[:, :])
                        ins.then_inc(small_ready, 1)
                    if step[0] == "C":
                        between(0, step[1] - 1, first=True)

            stage(PROLOGUE, 0, 0, 1, 0, 0)
            pe.wait_ge(ops_filled, 5)
            with pe.Fori(0, GROUPS // 2 - 1) as i:
                stage(STEADY, i * 2 + 1, 1, i + 1, i + 1, i * (2 * SMALL) + SMALL_0)
                stage(STEADY, i * 2 + 2, 0, i + 2, i + 1, i * (2 * SMALL) + (SMALL_0 + SMALL))
            stage(STEADY, GROUPS - 1, 1, GROUPS // 2, GROUPS // 2, SMALL_0 + (GROUPS - 2) * SMALL)

            def between(ch, r, first=False):
                turns = bank[0] if first else bank[7]
                if r == 0:
                    pe.wait_ge(c_mg, ch + 1)
                    pe.wait_ge(c_top, 1 + ch)
                    for i in range(TI):
                        ins = pe.transpose(turns[:, i * P:(i + 1) * P], mg_w[:, i * P:(i + 1) * P], ident[:, :])
                    ins.then_inc(c_mgt, 1)
                if r == 1:
                    pe.wait_ge(c_mgs, 1 + ch + 1)
                    for i in range(TI):
                        ins = pe.matmul(turns[:, i * D:(i + 1) * D], mg_t[:, i * P:(i + 1) * P], wo[:, :],
                                        start=True, stop=True)
                    ins.then_inc(c_y, 1)
                if r == 6:
                    pe.wait_ge(c_x1, 1 + ch + 1)
                    for i in range(TI):
                        ins = pe.transpose(turns[:, i * P:(i + 1) * P], x1_w[:, i * P:(i + 1) * P], ident[:, :])
                    ins.then_inc(c_x1t, 1)
                if r == 8:
                    pe.wait_ge(c_x1s, ch + 1)
                    for i in range(TI):
                        ins = pe.matmul(turns[:, i * E:(i + 1) * E], x1_tw[:, i * P:(i + 1) * P], rw[:, :],
                                        start=True, stop=True)
                    ins.then_inc(c_log, 1)

            def experts(ch, n):
                if n < UNITS:
                    if n == 0:
                        pe.wait_ge(c_lo, 1 + ch + 1)
                    pe.wait_ge(f_hid, ch * UNITS + n + 1)
                    for w in range(2):
                        at = slice(w * E * F + n * P, w * E * F + (n + 1) * P)
                        for k, (ws, xs) in enumerate(((w_hi, x1_hi), (w_hi, x1_lo), (w_lo, x1_hi))):
                            ins = pe.matmul(bank[2 * (n % 2) + w][:, :], ws[:, at], xs[:, bass.ds(ch * CH, CH)],
                                            start=k == 0, stop=k == 2)
                    ins.then_inc(f_ab, 1)
                if W2_LAG <= n < UNITS + W2_LAG:
                    m = n - W2_LAG
                    e, f = divmod(m, FT)
                    if f == 0:
                        pe.wait_ge(f_eo, ch * E + e + 1)
                    pe.wait_ge(f_lo, ch * UNITS + m + 1 + HB)
                    at = slice(2 * E * F + m * P, 2 * E * F + (m + 1) * P)
                    for k, (ws, hs) in enumerate(((w_hi, hid_hi), (w_hi, hid_lo), (w_lo, hid_hi))):
                        ins = pe.matmul(bank[4 + e % 2][:, :], ws[:, at], hs[:, m % HB, :],
                                        start=f == 0 and k == 0, stop=f == FT - 1 and k == 2)
                    ins.then_inc(f_w2, 1)
                if n >= TR_STEP and (n - TR_STEP) % FT == 0 and n < TR_STEP + UNITS:
                    e = (n - TR_STEP) // FT
                    pe.wait_ge(f_eo, ch * E + e + 1 + 2)
                    pe.wait_ge(f_y, 1 + ch * E + e)
                    for i in range(TI):
                        ins = pe.transpose(bank[6][:, i * P:(i + 1) * P], eo_sb[:, e % 2, i * P:(i + 1) * P],
                                           ident[:, :])
                    ins.then_inc(f_tr, 1)

            pe.wait_ge(s_reduced, SB + NS * GROUPS)
            pe.wait_ge(w_split, 1 + GROUPS - 2)
            pe.wait_ge(ld_small, 16 * 6)
            stage(LAST, GROUPS, 0, 0, GROUPS // 2, SMALL_0 + (GROUPS - 1) * SMALL)
            pe.wait_ge(c_top, 2)
            pe.sem_inc(f_w2, HB)
            pe.sem_inc(f_tr, 2)
            for n in range(HEAD):
                experts(0, n)
            pe.wait_ge(small_read, SMALL_0 + GROUPS * SMALL)
            with pe.Fori(0, CHUNKS - 1) as i:
                for n in range(HEAD, HEAD + UNITS):
                    if n >= UNITS:
                        experts(i + 1, n - UNITS)
                    experts(i, n)
                    between(i + 1, n - HEAD)
            for n in range(HEAD, Z_STEP + 1):
                experts(CHUNKS - 1, n)


def kernel(**inputs):
    import concourse.bacc as bacc
    from concourse.bass_utils import run_bass_kernel_spmd

    x = np.ascontiguousarray(inputs["L0_attn_x"])
    tokens = x.reshape(T, D)
    w1 = inputs["L0_ffn_w1"].transpose(1, 0, 2).reshape(D, E * F)
    w3 = inputs["L0_ffn_w3"].transpose(1, 0, 2).reshape(D, E * F)
    w2 = inputs["L0_ffn_w2"].reshape(E * FT, P, D).transpose(1, 0, 2).reshape(P, E * F)
    inv_freq = np.float32(1.0) / np.float32(10000.0) ** (np.arange(0, DH, 2, dtype=np.float32) / np.float32(DH))
    freq = (np.arange(S, dtype=np.float32)[:, None] * inv_freq[None, :]).astype(np.float32)
    row = (np.arange(D) % DH) // 2
    arrays = {
        "x_tok": tokens, "x_feat": np.ascontiguousarray(tokens.T),
        "qw": inputs["L0_attn_qw"], "kw": inputs["L0_attn_kw"], "vw": inputs["L0_attn_vw"], "ow": inputs["L0_attn_ow"],
        "router_w": inputs["L0_ffn_router_w"], "router_b": inputs["L0_ffn_router_b"],
        "w_all": np.concatenate([w1, w3, w2], axis=1),
        "cos_t": np.cos(freq).T[row], "sin_t": np.sin(freq).T[row],
        "ident": np.eye(P, dtype=np.float32),
        "mask": np.where(np.arange(QD)[None, :] > (np.arange(P) % QD)[:, None], np.float32(MASKED), np.float32(0)),
        "tri": np.broadcast_to(np.stack([np.triu(np.ones((E, E), np.float32), 1).ravel(),
                                         np.tril(np.ones((E, E), np.float32), -1).ravel()]), (P, 2, E * E)),
    }
    arrays = {n: np.ascontiguousarray(a) for n, a in arrays.items()}
    nc = bacc.Bacc("TRN2", target_bir_lowering=False, num_devices=1)
    args = [nc.dram_tensor(f"in_{n}", a.shape, mybir.dt.from_np(a.dtype), kind="ExternalInput").ap()
            for n, a in arrays.items()]
    out = nc.dram_tensor("out_tokens", (T, D), F32, kind="ExternalOutput").ap()
    transformer_block(nc, *args, out)
    r = run_bass_kernel_spmd(nc, [{f"in_{n}": a for n, a in arrays.items()}], core_ids=[0])
    return r.results[0]["out_tokens"].reshape(B, S, D)
```
